# Optimizing a Trainium2 kernel written in Bass

```python
import numpy as np
import jax
import jax.numpy as jnp

def _softmax(x, axis=-1):
    return jax.nn.softmax(x, axis=axis)

def _gelu(x):
    return jax.nn.gelu(x, approximate=True)

def _silu(x):
    return jax.nn.silu(x)

def _sigmoid(x):
    return jax.nn.sigmoid(x)

def _layernorm(x, axis=-1, eps=1e-05):
    m = jnp.mean(x, axis=axis, keepdims=True)
    v = jnp.var(x, axis=axis, keepdims=True)
    return (x - m) / jnp.sqrt(v + eps)

def _scatter_add(tgt, idx, src, axis=0):
    return tgt.at[idx].add(src)

def _segment_sum(src, seg, n):
    return jax.ops.segment_sum(src, seg, n)
kernel_name = 'mk_macaron_d1_jaxref_r8_930874'

def setup_inputs(seed: int=0):
    np.random.seed(seed)
    _w = jnp.asarray

    def _L0_attn_setup():
        import jax, jax.numpy as jnp
        import numpy as np
        DIM = 128
        HEADS = 16
        HEAD_DIM = DIM // HEADS
        ROPE_BASE = 500000.0
        SCALE = HEAD_DIM ** (-0.5)

        def _rope_cos_sin(T, dtype=jnp.float32):
            inv_freq = 1.0 / ROPE_BASE ** (jnp.arange(0, HEAD_DIM, 2, dtype=jnp.float32) / HEAD_DIM)
            t = jnp.arange(T, dtype=jnp.float32)
            freqs = t[:, None] * inv_freq[None, :]
            emb = jnp.concatenate([freqs, freqs], axis=-1)
            return (jnp.cos(emb).astype(dtype), jnp.sin(emb).astype(dtype))

        def _rotate_half(x):
            x1, x2 = jnp.split(x, 2, axis=-1)
            return jnp.concatenate([-x2, x1], axis=-1)

        def _apply_rope(x, cos, sin):
            return x * cos + _rotate_half(x) * sin
        key = jax.random.key(seed)
        k1, k2, k3 = jax.random.split(key, 3)
        B, T = (4, 512)
        x = jax.random.normal(k1, (B, T, DIM), dtype=jnp.float32)
        W_qkv = jax.random.normal(k2, (DIM, 3 * DIM), dtype=jnp.float32) * DIM ** (-0.5)
        W_out = jax.random.normal(k3, (DIM, DIM), dtype=jnp.float32) * DIM ** (-0.5)
        return {'x': x, 'W_qkv': W_qkv, 'W_out': W_out}
    _L0_attn_in = _L0_attn_setup()

    def _L0_ffn_setup():
        import jax, jax.numpy as jnp
        import numpy as np
        N_EMBD = 128
        EXPERT_SIZES = [(4, 128), (4, 256)]
        TOP_K = 2
        B, S = (1, 256)
        WIDTHS = []
        for count, size in EXPERT_SIZES:
            WIDTHS += [size] * count
        OFFSETS = np.concatenate([[0], np.cumsum(WIDTHS)]).astype(np.int64)
        E = len(WIDTHS)
        TOTAL_W = int(OFFSETS[-1])
        MAX_W = max(WIDTHS)

        def _stack_experts(w1, w2):
            W1e, W2e = ([], [])
            for e in range(E):
                off, wd = (int(OFFSETS[e]), WIDTHS[e])
                pad = MAX_W - wd
                W1e.append(jnp.pad(w1[:, off:off + wd], ((0, 0), (0, pad))))
                W2e.append(jnp.pad(w2[off:off + wd, :], ((0, pad), (0, 0))))
            return (jnp.stack(W1e), jnp.stack(W2e))
        key = jax.random.key(seed)
        k1, k2, k3, k4 = jax.random.split(key, 4)
        x = jax.random.normal(k1, (B, S, N_EMBD), jnp.float32)
        router_w = jax.random.normal(k2, (E, N_EMBD), jnp.float32) * 0.02
        w1 = jax.random.truncated_normal(k3, -3.0, 3.0, (N_EMBD, TOTAL_W), jnp.float32) * 0.02
        w2 = jax.random.truncated_normal(k4, -3.0, 3.0, (TOTAL_W, N_EMBD), jnp.float32) * 0.02
        return {'x': x, 'router_w': router_w, 'w1': w1, 'w2': w2}
    _L0_ffn_in = _L0_ffn_setup()
    _d = {'L0_attn_x': _L0_attn_in['x'], 'L0_attn_W_qkv': _L0_attn_in['W_qkv'], 'L0_attn_W_out': _L0_attn_in['W_out'], 'L0_ffn_router_w': _L0_ffn_in['router_w'], 'L0_ffn_w1': _L0_ffn_in['w1'], 'L0_ffn_w2': _L0_ffn_in['w2']}
    _x0 = _d['L0_attn_x']
    _d['L0_attn_x'] = jax.random.normal(jax.random.fold_in(jax.random.key(seed), 1), (32, 256, 128), dtype=_x0.dtype)
    del _x0
    return _d

def reference(L0_attn_x, L0_attn_W_qkv, L0_attn_W_out, L0_ffn_router_w, L0_ffn_w1, L0_ffn_w2):

    def _L0_attn_ref(x, W_qkv, W_out):
        import jax, jax.numpy as jnp
        import numpy as np
        DIM = 128
        HEADS = 16
        HEAD_DIM = DIM // HEADS
        ROPE_BASE = 500000.0
        SCALE = HEAD_DIM ** (-0.5)

        def _rope_cos_sin(T, dtype=jnp.float32):
            inv_freq = 1.0 / ROPE_BASE ** (jnp.arange(0, HEAD_DIM, 2, dtype=jnp.float32) / HEAD_DIM)
            t = jnp.arange(T, dtype=jnp.float32)
            freqs = t[:, None] * inv_freq[None, :]
            emb = jnp.concatenate([freqs, freqs], axis=-1)
            return (jnp.cos(emb).astype(dtype), jnp.sin(emb).astype(dtype))

        def _rotate_half(x):
            x1, x2 = jnp.split(x, 2, axis=-1)
            return jnp.concatenate([-x2, x1], axis=-1)

        def _apply_rope(x, cos, sin):
            return x * cos + _rotate_half(x) * sin
        B, T, D = x.shape
        H, hd = (HEADS, HEAD_DIM)
        qkv = (x @ W_qkv).reshape(B, T, 3, H, hd).transpose(2, 0, 3, 1, 4)
        q, k, v = (qkv[0], qkv[1], qkv[2])
        cos, sin = _rope_cos_sin(T, q.dtype)
        q = _apply_rope(q, cos, sin)
        k = _apply_rope(k, cos, sin)
        q_feat = jax.nn.elu(q * SCALE) + 1.0
        k_feat = jax.nn.elu(k) + 1.0
        kv = jnp.einsum('bhtd,bhtv->bhdv', k_feat, v)
        k_sum = k_feat.sum(axis=2)
        denom = jnp.maximum(jnp.einsum('bhtd,bhd->bht', q_feat, k_sum), 1e-06)
        out = jnp.einsum('bhtd,bhdv->bhtv', q_feat, kv) / denom[..., None]
        out = out.transpose(0, 2, 1, 3).reshape(B, T, D)
        return out @ W_out

    def _L0_ffn_ref(x, router_w, w1, w2):
        import jax, jax.numpy as jnp
        import numpy as np
        N_EMBD = 128
        EXPERT_SIZES = [(4, 128), (4, 256)]
        TOP_K = 2
        B, S = (1, 256)
        WIDTHS = []
        for count, size in EXPERT_SIZES:
            WIDTHS += [size] * count
        OFFSETS = np.concatenate([[0], np.cumsum(WIDTHS)]).astype(np.int64)
        E = len(WIDTHS)
        TOTAL_W = int(OFFSETS[-1])
        MAX_W = max(WIDTHS)

        def _stack_experts(w1, w2):
            W1e, W2e = ([], [])
            for e in range(E):
                off, wd = (int(OFFSETS[e]), WIDTHS[e])
                pad = MAX_W - wd
                W1e.append(jnp.pad(w1[:, off:off + wd], ((0, 0), (0, pad))))
                W2e.append(jnp.pad(w2[off:off + wd, :], ((0, pad), (0, 0))))
            return (jnp.stack(W1e), jnp.stack(W2e))
        b, s, d = x.shape
        xf = x.reshape(-1, d)
        logits = xf @ router_w.T
        probs = jax.nn.sigmoid(logits.astype(jnp.float32))
        topw, sel = jax.lax.top_k(probs, TOP_K)
        topw = topw / (topw.sum(-1, keepdims=True) + 1e-20)
        topw = topw.astype(x.dtype)
        onehot = sel[:, :, None] == jnp.arange(E)[None, None, :]
        combine = jnp.sum(topw[:, :, None] * onehot, axis=1)
        W1e, W2e = _stack_experts(w1, w2)
        h = jnp.einsum('td,edw->tew', xf, W1e)
        h = jnp.square(jax.nn.relu(h))
        y = jnp.einsum('tew,ewd->ted', h, W2e)
        out = jnp.einsum('ted,te->td', y, combine)
        return out.reshape(b, s, d)
    x = L0_attn_x
    x = x + 0.5 * _L0_ffn_ref(_layernorm(x, axis=-1), L0_ffn_router_w, L0_ffn_w1, L0_ffn_w2)
    x = x + _L0_attn_ref(_layernorm(x, axis=-1), L0_attn_W_qkv, L0_attn_W_out)
    x = x + 0.5 * _L0_ffn_ref(_layernorm(x, axis=-1), L0_ffn_router_w, L0_ffn_w1, L0_ffn_w2)
    return x

_drawn_inputs = setup_inputs


def setup_inputs(seed=0):
    import zlib

    import numpy as np

    out = dict(_drawn_inputs(seed))
    spreads = {}
    factors = {'L0_ffn_router_w': 5.616, 'L0_ffn_w1': 5.345, 'L0_ffn_w2': 4.917}
    for name, (base, spread) in spreads.items():
        noise = np.random.default_rng([zlib.crc32(name.encode()), seed]).standard_normal(out[name].shape)
        drawn = base * np.exp(spread * noise) if base else spread * noise
        out[name] = jnp.asarray(drawn.astype(out[name].dtype))
    for name, factor in factors.items():
        out[name] = (out[name] * factor).astype(out[name].dtype)
    return out
```

```python
from contextlib import ExitStack

import numpy as np

import concourse.bass as bass
from concourse import mybir

F32 = mybir.dt.float32
F32R = mybir.dt.float32r
ALU = mybir.AluOpType
ACT = mybir.ActivationFunctionType
AX = mybir.AxisListType

B, T, D = 32, 256, 128
P = 128
RT = T // P
BG = 2
TG = BG * RT
NTOK = TG * P
NG = B // BG
NT = B * RT
HEADS, HD = 16, 8
HALF = HD // 2
WIDTHS = [128] * 4 + [256] * 4
EXP = len(WIDTHS)
WTOT = sum(WIDTHS)
NC = WTOT // P
CQ = NC // TG
TOPK = 2
EH = EXP // 2
KVW = D + HEADS
ROPE_BASE = 500000.0
EPS = 1e-5
SHIFT = 7
T_FIRST, T_LAST = -3, NG + SHIFT - 1

CHUNKS = []
for w_ in WIDTHS:
    CHUNKS.append((sum(k for _, k in CHUNKS), w_ // P))


class Step:

    def __init__(self, i, a, c, trips):
        self.i, self.a, self.c, self.trips = i, a, c, trips

    def __add__(self, k):
        return Step(self.i, self.a, self.c + k, self.trips)

    def __sub__(self, k):
        return self + (-k)

    def __mul__(self, k):
        return Step(self.i, self.a * k, self.c * k, self.trips)

    @property
    def last(self):
        return self.c + self.a * (self.trips - 1)

    @property
    def value(self):
        return self.i * self.a + self.c


def first(v):
    return v.c if isinstance(v, Step) else v


def last(v):
    return v.last if isinstance(v, Step) else v


def value(v):
    return v.value if isinstance(v, Step) else v


def due(v):
    assert (first(v) > 0) == (last(v) > 0)
    return first(v) > 0


def live(n):
    return first(n) >= 0 and last(n) < NG


def first_time(stream, n):
    return stream and not isinstance(n, Step) and n == 0


def done(n):
    if last(n) <= 0:
        return 0
    if first(n) >= NG:
        return NG
    assert first(n) >= 0 and last(n) <= NG
    return n


def stages(t):
    ns = [t + 3, t + 2, t + 1, t, t - 1, t - 2, t - 3]
    ns += [t + 3 - SHIFT, t + 2 - SHIFT, t + 1 - SHIFT, t - SHIFT]
    return tuple((n >= 0) + (n > 0) + (n >= NG) for n in ns)


def runs():
    out = []
    for t in range(T_FIRST, T_LAST + 1, 2):
        kind = (stages(t), stages(t + 1))
        if out and out[-1][2] == kind and kind[0] == kind[1]:
            out[-1][1] += 1
        else:
            out.append([t, 1, kind])
    return [(t, trips) for t, trips, _ in out]


def pipeline(eng, iteration):
    for t0, trips in runs():
        if trips == 1:
            for u in range(2):
                iteration(t0 + u, (t0 + u) % 2)
        else:
            with eng.Fori(0, trips) as i:
                for u in range(2):
                    iteration(Step(i, 2, t0 + u, trips), (t0 + u) % 2)


def constant_columns():
    inv = (1.0 / ROPE_BASE ** (np.arange(0, HD, 2, dtype=np.float32) / np.float32(HD))).astype(np.float32)
    ang = np.arange(T, dtype=np.float32)[:, None] * inv[None, :]
    cos, sin = np.cos(ang).astype(np.float32), np.sin(ang).astype(np.float32)
    col_f = np.arange(D) % HALF
    sign = np.where(np.arange(D) < D // 2, -1.0, 1.0).astype(np.float32)
    cos_k, sin_k = cos[:, col_f], sin[:, col_f] * sign
    scale = np.float32(HD ** -0.5)
    tok = (RT * np.arange(P)[None, :] + np.arange(RT)[:, None]).ravel()
    head_qk = (np.arange(D) % (D // 2)) // HALF
    head_v = np.arange(D) // HD
    a, b = np.arange(EXP)[:, None], np.arange(EXP)[None, :]
    parts = {
        "ident": np.eye(P),
        "cos_q": cos_k[tok].T * scale,
        "sin_q": sin_k[tok].T * scale,
        "cos_k": cos_k.reshape(P, RT * D),
        "sin_k": sin_k.reshape(P, RT * D),
        "same_head": head_qk[:, None] == head_v[None, :],
        "in_head": head_qk[:, None] == np.arange(HEADS)[None, :],
        "before": np.broadcast_to((b < a).reshape(1, EXP * EXP), (P, EXP * EXP)),
        "after": np.broadcast_to(EXP - 1 - np.arange(EXP)[None, :], (P, EXP)),
    }
    where, at = {}, 0
    for name, v in parts.items():
        where[name] = (at, at + v.shape[1])
        at += v.shape[1]
    return np.concatenate([np.asarray(v, np.float32) for v in parts.values()], 1), where


CONST, WHERE = constant_columns()


def build(nc, x_in, wqkv, wout, router, w1, w2, const, out):
    ctx = ExitStack()
    with ctx:
        def sb(name, shape, dt=F32):
            return ctx.enter_context(nc.sbuf_tensor(name, shape, dt))

        def sem(name):
            return ctx.enter_context(nc.semaphore(name))

        FFN = ("f1", "f2")
        STREAMS = ("f1", "at", "f2")

        x_sb = sb("x_sb", [P, NT, D])
        con = sb("con", [P, CONST.shape[1]])
        w1_hi = sb("w1_hi", [P, WTOT], F32R)
        w1_lo = sb("w1_lo", [P, WTOT], F32R)
        w2_sb = sb("w2_sb", [P, NC, D])
        router_sb = sb("router_sb", [P, P])
        wq_hi, wq_lo = sb("wq_hi", [P, 2, D], F32R), sb("wq_lo", [P, 2, D], F32R)
        wkv_hi, wkv_lo = sb("wkv_hi", [P, 2 * D], F32R), sb("wkv_lo", [P, 2 * D], F32R)
        wout_sb = sb("wout_sb", [P, D])
        h_sb = {s: [sb(f"h_{s}{u}", [P, NC, NTOK]) for u in range(2)] for s in FFN}
        early = h_sb["f2"][0][:].rearrange("p c t -> p (c t)")
        w1_raw, wqkv_raw = early[:, 0:WTOT], early[:, WTOT:WTOT + 3 * D]
        xn = {s: sb(f"xn_{s}", [P, TG, D]) for s in STREAMS}
        xT = sb("xT", [P, NTOK])
        xT = {s: xT for s in STREAMS}
        nx = {"f1": 2, "at": 1, "f2": 2}
        x_hi = {s: [sb(f"x_hi_{s}{u}", [P, NTOK], F32R) for u in range(nx[s])] for s in STREAMS}
        x_lo = {s: [sb(f"x_lo_{s}{u}", [P, NTOK], F32R) for u in range(nx[s])] for s in STREAMS}
        bn = {s: sb(f"bn_{s}", [P, TG, 6]) for s in STREAMS}
        mv = {s: sb(f"mv_{s}", [P, TG, 2]) for s in STREAMS}
        ve = {s: sb(f"ve_{s}", [P, TG]) for s in STREAMS}
        nm = {s: sb(f"nm_{s}", [P, TG]) for s in STREAMS}
        rstd = {s: sb(f"rstd_{s}", [P, TG]) for s in STREAMS}
        nbias = {s: sb(f"nbias_{s}", [P, TG]) for s in STREAMS}
        c_eps, c_mhalf, c_mone = sb("c_eps", [P, TG]), sb("c_mhalf", [P, TG]), sb("c_mone", [P, TG])
        ex = {s: sb(f"ex_{s}", [P, TG, EXP]) for s in FFN}
        prob = {s: sb(f"prob_{s}", [P, TG, EXP]) for s in FFN}
        geq = {s: sb(f"geq_{s}", [P, TG, EXP, EXP]) for s in FFN}
        ahead = {s: sb(f"ahead_{s}", [P, TG, EXP, EXP + 1]) for s in FFN}
        r1 = {s: sb(f"r1_{s}", [P, TG, EXP]) for s in FFN}
        r2 = {s: sb(f"r2_{s}", [P, TG, EXP]) for s in FFN}
        chosen = {s: sb(f"chosen_{s}", [P, TG, EXP]) for s in FFN}
        tot = {s: sb(f"tot_{s}", [P, TG]) for s in FFN}
        cw = {s: [sb(f"cw_{s}{u}", [P, TG, EXP]) for u in range(2)] for s in FFN}
        prod = [sb(f"prod{i}", [P, EXP, D]) for i in range(2)]
        t1, t2, t3 = sb("t1", [P, EXP // 2, D]), sb("t2", [P, EXP // 4, D]), sb("t3", [P, D])
        qa, qb = sb("qa", [P, BG, T]), sb("qb", [P, BG, T])
        eq = qb
        qf = sb("qf", [P, NTOK])
        ka, kb = sb("ka", [P, TG, D]), sb("kb", [P, TG, D])
        ek = kb
        kf = sb("kf", [P, TG, D])
        v_sb = sb("v_sb", [P, TG, D + 1])
        kvm = sb("kvm", [P, BG, KVW])
        den = sb("den", [P, TG, HEADS])
        rden = sb("rden", [P, TG, HEADS])
        attn = sb("attn", [P, TG, D])
        attnT = attn[:].rearrange("p k d -> p (k d)")

        def cc(name):
            a, b = WHERE[name]
            return con[:, a:b]

        ident = cc("ident")
        cos_q = cc("cos_q").unsqueeze(1).to_broadcast([P, BG, T])
        sin_q = cc("sin_q").unsqueeze(1).to_broadcast([P, BG, T])
        cos_k = cc("cos_k").rearrange("p (r d) -> p r d", r=RT)
        sin_k = cc("sin_k").rearrange("p (r d) -> p r d", r=RT)
        same_head = cc("same_head").unsqueeze(1).to_broadcast([P, BG, D])
        in_head = cc("in_head").unsqueeze(1).to_broadcast([P, BG, HEADS])
        before = cc("before").rearrange("p (a b) -> p a b", a=EXP)
        after = cc("after")

        bank = [ctx.enter_context(nc.psum_tensor(f"bank{i}", [P, 512], F32)) for i in range(8)]
        tp = bank[0]
        hp = bank[1:3]
        yp = bank[3:5]
        a0, a1, a2 = bank[5:8]

        s_load = [sem(f"s_load{u}") for u in range(2)]
        s_w1, s_w2, s_con, s_wqkv, s_router, s_wout = (
            sem(n) for n in ("s_w1", "s_w2", "s_con", "s_wqkv", "s_router", "s_wout"))
        s_store = sem("s_store")
        s_gate = sem("s_gate")
        s_w1hi, s_w1lo, s_wa_hi, s_wa_lo = (sem(n) for n in ("s_w1hi", "s_w1lo", "s_wa_hi", "s_wa_lo"))
        s_zero, s_pconst, s_set = sem("s_zero"), sem("s_pconst"), sem("s_set")

        def per(name, keys):
            return {s: sem(f"s_{name}_{s}") for s in keys}

        s_bn = per("bn", STREAMS)
        s_mv = per("mv", STREAMS)
        s_ve = per("ve", STREAMS)
        s_rstd = per("rstd", STREAMS)
        s_nb = per("nb", STREAMS)
        s_xn = per("xn", STREAMS)
        s_t = per("t", STREAMS)
        s_xT = per("xT", STREAMS)
        s_hi = per("hi", STREAMS)
        s_lo = per("lo", STREAMS)
        s_logit = per("logit", FFN)
        s_ex = per("ex", FFN)
        s_rt = per("rt", FFN)
        s_geq = per("geq", FFN)
        s_ahead = per("ahead", FFN)
        s_cw = per("cw", FFN)
        s_p1 = per("p1", FFN)
        s_relu = per("relu", FFN)
        s_sq = per("sq", FFN)
        s_p2 = per("p2", FFN)
        s_prod = per("prod", FFN)
        s_t1, s_t2, s_t3 = per("t1", FFN), per("t2", FFN), per("t3", FFN)
        s_x = per("x", FFN)
        names = "q qr qa qb xq eq qf kv ka kb v xk ek kf state kvm kvs nd den rden attn at atT y x2".split()
        A = {n: sem(f"s_a_{n}") for n in names}
        RSTEPS = 8
        other = {"f1": "f2", "f2": "f1"}
        off = {"f1": 0, "f2": SHIFT}

        def through(o, s, t):
            return done(t + (1 if s == "f2" else 0) - off[o])

        x_dram = x_in.rearrange("b (p r) d -> p b (r d)", r=RT)
        o_dram = out.rearrange("b (p r) d -> p b (r d)", r=RT)
        x_rows = x_sb[:].rearrange("p (b r) d -> p b (r d)", r=RT)

        block = ctx.enter_context(nc.Block())

        @block.sync
        def _(sp):
            def load(n, u):
                if due((n - u) * 8):
                    sp.wait_ge(s_load[u], value((n - u) * 8))
                g = value(n)
                sp.dma_start(x_rows[:, bass.ds(g * BG, BG), :], x_dram[:, bass.ds(g * BG, BG), :]) \
                    .then_inc(s_load[u], 16)

            for u in range(2):
                load(u, u)
            with sp.Fori(0, NG // 2 - 1) as i:
                for u in range(2):
                    load(Step(i, 2, 2 + u, NG // 2 - 1), u)
            with sp.Fori(0, NG) as i:
                n = Step(i, 1, 0, NG)
                sp.wait_ge(s_x["f2"], value(n * TG + TG))
                g = value(n)
                sp.dma_start(o_dram[:, bass.ds(g * BG, BG), :], x_rows[:, bass.ds(g * BG, BG), :]) \
                    .then_inc(s_store, 16)
            sp.wait_ge(s_store, NG * 16)

        @block.tensor
        def _(pe):
            mm = nc.tensor.matmul

            def tp_free(t, pos):
                n1, na, n2 = t + 2, t - 2, t + 2 - SHIFT
                if pos > 0:
                    n1 += 1
                if pos > 1:
                    na += 1
                if due(done(n1)):
                    pe.wait_ge(s_ex["f1"], value(done(n1)))
                if due(done(na)):
                    pe.wait_ge(s_xT["at"], value(done(na)))
                if due(done(n2)):
                    pe.wait_ge(s_ex["f2"], value(done(n2)))

            def transpose(s, n, t, pos):
                if not live(n):
                    return
                pe.wait_ge(s_xn[s], value(n + 1))
                tp_free(t, pos)
                for k in range(TG):
                    i = nc.tensor.transpose(tp[:, k * P:(k + 1) * P], xn[s][:, k, :], ident)
                i.then_inc(s_t[s], 1)

            def logits(s, n):
                if not live(n):
                    return
                pe.wait_ge(s_xT[s], value(n + 1))
                if first_time(s == "f1", n):
                    pe.wait_ge(s_router, 16)
                for k in range(TG):
                    i = mm(tp[:, k * P:(k + 1) * P], xT[s][:, k * P:(k + 1) * P], router_sb[:], start=True, stop=True)
                i.then_inc(s_logit[s], 1)

            def up(s, n, c, u, t):
                if not live(n):
                    return
                if c == 0:
                    pe.wait_ge(s_lo[s], value(n + 1))
                    if first_time(s == "f1", n):
                        pe.wait_ge(s_w1lo, 1)
                if c < 2:
                    m = through(other[s], s, t + 1) * NC
                    if due(m):
                        pe.wait_ge(s_relu[other[s]], value(m))
                m = n * NC + max(c - 1, 0)
                if due(m):
                    pe.wait_ge(s_relu[s], value(m))
                w = slice(c * P, (c + 1) * P)
                o = hp[c % 2][:]
                mm(o, w1_hi[:, w], x_hi[s][u][:], start=True, stop=False)
                mm(o, w1_hi[:, w], x_lo[s][u][:], start=False, stop=False)
                mm(o, w1_lo[:, w], x_hi[s][u][:], start=False, stop=True).then_inc(s_p1[s], 1)

            def down(s, n, j, half, u, t):
                if not live(n):
                    return
                if j == 0 and half == 0:
                    pe.wait_ge(s_sq[s], value(n * TG + TG))
                    if first_time(s == "f1", n):
                        pe.wait_ge(s_w2, 16)
                if j == 0:
                    m = through(other[s], s, t) * (2 * TG)
                    if due(m):
                        pe.wait_ge(s_prod[other[s]], value(m))
                m = n * (2 * TG) + (2 * j + half - 1)
                if due(m):
                    pe.wait_ge(s_prod[s], value(m))
                for e in range(half * EH, (half + 1) * EH):
                    c0, k = CHUNKS[e]
                    for c in range(c0, c0 + k):
                        i = mm(yp[half][:, (e % EH) * D:(e % EH + 1) * D], h_sb[s][u][:, c, j * P:(j + 1) * P],
                               w2_sb[:, c, :], start=(c == c0), stop=(c == c0 + k - 1))
                i.then_inc(s_p2[s], 1)

            def quarter(s, t, j, par):
                n2 = t - off[s]
                u = (par + off[s]) % 2
                up(s, n2 + 1, CQ * j, 1 - u, t)
                up(s, n2 + 1, CQ * j + 1, 1 - u, t)
                down(s, n2, j, 0, u, t)
                up(s, n2 + 1, CQ * j + 2, 1 - u, t)
                down(s, n2, j, 1, u, t)

            def split_product(o, parts):
                for k, (a, b) in enumerate(parts):
                    i = mm(o, a, b, start=(k == 0), stop=(k == len(parts) - 1))
                return i

            def q_proj(n, rot, o):
                hi, lo = x_hi["at"][0][:], x_lo["at"][0][:]
                return split_product(o, [(wq_hi[:, rot, :], hi), (wq_hi[:, rot, :], lo), (wq_lo[:, rot, :], hi)])

            def q(n):
                if not live(n):
                    return
                pe.wait_ge(s_lo["at"], value(n + 1))
                if first_time(True, n):
                    pe.wait_ge(s_wa_lo, 1)
                if due(n):
                    pe.wait_ge(A["attn"], value(n))
                q_proj(n, 0, a0[:]).then_inc(A["q"], 1)

            def q_rotated(n):
                if not live(n):
                    return
                if due(n):
                    pe.wait_ge(A["atT"], value(n))
                q_proj(n, 1, a1[:]).then_inc(A["qr"], 1)

            def kv(n, b):
                if not live(n):
                    return
                if b == 0:
                    if due(n):
                        pe.wait_ge(A["x2"], value(n))
                else:
                    pe.wait_ge(A["qa"], value(n + 1))
                for r in range(RT):
                    c = slice((b * RT + r) * P, (b * RT + r + 1) * P)
                    hi, lo = x_hi["at"][0][:, c], x_lo["at"][0][:, c]
                    i = split_product((a2, a0)[b][:, r * 2 * D:(r + 1) * 2 * D],
                                      [(hi, wkv_hi[:]), (lo, wkv_hi[:]), (hi, wkv_lo[:])])
                i.then_inc(A["kv"], 1)

            def state(n):
                if not live(n):
                    return
                pe.wait_ge(A["kf"], value(n + 1))
                if first_time(True, n):
                    pe.wait_ge(s_set, 1)
                pe.wait_ge(A["v"], value(n * BG + BG))
                for b in range(BG):
                    for r in range(RT):
                        k = b * RT + r
                        i = mm(a1[:, b * 2 * D:b * 2 * D + D + 1], kf[:, k, :], v_sb[:, k, :],
                               start=(r == 0), stop=(r == RT - 1))
                i.then_inc(A["state"], 1)

            def attend(n):
                if not live(n):
                    return
                pe.wait_ge(A["qf"], value(n + 1))
                pe.wait_ge(A["kvs"], value(n + 1))
                for b in range(BG):
                    for r in range(RT):
                        k = b * RT + r
                        i = mm((a2, a0)[b][:, r * 2 * D:r * 2 * D + KVW], qf[:, k * P:(k + 1) * P],
                               kvm[:, b, :], start=True, stop=True)
                i.then_inc(A["nd"], 1)

            def attn_transpose(n):
                if not live(n):
                    return
                pe.wait_ge(A["attn"], value(n + 1))
                for k in range(TG):
                    i = nc.tensor.transpose(a1[:, k * P:(k + 1) * P], attn[:, k, :], ident)
                i.then_inc(A["at"], 1)

            def out_proj(n):
                if not live(n):
                    return
                pe.wait_ge(A["atT"], value(n + 1))
                if first_time(True, n):
                    pe.wait_ge(s_wout, 16)
                for k in range(TG):
                    i = mm(a2[:, k * D:(k + 1) * D], attnT[:, k * P:(k + 1) * P], wout_sb[:], start=True, stop=True)
                i.then_inc(A["y"], 1)

            pe.wait_ge(s_con, 16)

            def iteration(t, par):
                transpose("f1", t + 2, t, 0)
                quarter("f1", t, 0, par)
                state(t - 3)
                logits("f1", t + 2)
                quarter("f1", t, 1, par)
                attend(t - 3)
                quarter("f1", t, 2, par)
                attn_transpose(t - 3)
                transpose("at", t - 2, t, 1)
                quarter("f1", t, 3, par)
                out_proj(t - 3)
                transpose("f2", t + 2 - SHIFT, t, 2)
                quarter("f2", t, 0, par)
                q(t - 2)
                logits("f2", t + 2 - SHIFT)
                quarter("f2", t, 1, par)
                q_rotated(t - 2)
                quarter("f2", t, 2, par)
                kv(t - 2, 0)
                kv(t - 2, 1)
                quarter("f2", t, 3, par)

            pipeline(pe, iteration)

        @block.scalar
        def _(act):
            fn = nc.scalar.activation
            act.dma_start(w1_raw, w1).then_inc(s_w1, 16)
            act.dma_start(con[:], const).then_inc(s_con, 16)
            act.wait_ge(s_zero, 1)
            act.dma_start(router_sb[:, 0:EXP], router).then_inc(s_router, 16)
            act.dma_start(w2_sb[:], w2.rearrange("(c p) d -> p c d", p=P)).then_inc(s_w2, 16)
            act.dma_start(wqkv_raw, wqkv).then_inc(s_wqkv, 16)
            act.dma_start(wout_sb[:], wout).then_inc(s_wout, 16)

            def norm(s, n):
                if not live(n):
                    return
                act.wait_ge(s_nb[s], value(n + 1))
                if due(n):
                    act.wait_ge(s_t[s], value(n))
                for k in range(TG):
                    tile = x_sb[:, bass.ds(value(n * TG + k), 1), :].rearrange("p a d -> p (a d)")
                    i = fn(xn[s][:, k, :], tile, ACT.Identity, bias=nbias[s][:, k:k + 1], scale=rstd[s][:, k:k + 1])
                i.then_inc(s_xn[s], 1)

            def evacuate_x(s, n, t, pos):
                if not live(n):
                    return
                act.wait_ge(s_t[s], value(n + 1))
                for q, m in (("f1", t + 2), ("at", t - 2), ("f2", t + 2 - SHIFT)):
                    m = done(m + 1 if STREAMS.index(q) < pos else m)
                    if due(m):
                        act.wait_ge(s_lo[q], value(m))
                fn(xT[s][:], tp[:], ACT.Copy).then_inc(s_xT[s], 1)

            def exp_logits(s, n):
                if not live(n):
                    return
                act.wait_ge(s_logit[s], value(n + 1))
                if due(n * RSTEPS):
                    act.wait_ge(s_rt[s], value(n * RSTEPS))
                l = tp[:].rearrange("p (k e) -> p k e", k=TG)[:, :, 0:EXP]
                fn(ex[s][:], l, ACT.Exp, scale=-1.0).then_inc(s_ex[s], 1)

            def hidden(s, t, j, par):
                n = t + 1 - off[s]
                if not live(n):
                    return
                u = (par + 1 + off[s]) % 2
                for c in range(CQ * j, CQ * (j + 1)):
                    act.wait_ge(s_p1[s], value(n * NC + c + 1))
                    fn(h_sb[s][u][:, c, :], hp[c % 2][:], ACT.Relu).then_inc(s_relu[s], 1)
                act.wait_ge(s_relu[s], value(n * NC + CQ * (j + 1)))
                h = h_sb[s][u][:, CQ * j:CQ * (j + 1), :]
                fn(h, h, ACT.Square).then_inc(s_sq[s], 1)

            def exp_q(n):
                if live(n):
                    act.wait_ge(A["xq"], value(n + 1))
                    fn(eq[:], qa[:], ACT.Exp, bias=minus_one[:, 0:1]).then_inc(A["eq"], 1)

            def exp_k(n):
                if live(n):
                    act.wait_ge(A["xk"], value(n + 1))
                    fn(ek[:], ka[:], ACT.Exp, bias=minus_one[:, 0:1]).then_inc(A["ek"], 1)

            def copy_v(n):
                if not live(n):
                    return
                for b in range(BG):
                    act.wait_ge(A["kb"], value(n * BG + b + 1))
                    if b == 0:
                        if due(n):
                            act.wait_ge(A["state"], value(n))
                    src = (a2, a0)[b][:].rearrange("p (r c) -> p r c", r=RT)[:, :, D:2 * D]
                    fn(v_sb[:, b * RT:(b + 1) * RT, 0:D], src, ACT.Copy).then_inc(A["v"], 1)

            def copy_attnT(n):
                if live(n):
                    act.wait_ge(A["at"], value(n + 1))
                    fn(attnT, a1[:], ACT.Copy).then_inc(A["atT"], 1)

            act.wait_ge(s_pconst, 1)

            def iteration(t, par):
                evacuate_x("f1", t + 2, t, 0)
                hidden("f1", t, 0, par)
                exp_logits("f1", t + 2)
                norm("at", t - 2)
                hidden("f1", t, 1, par)
                norm("f2", t + 2 - SHIFT)
                hidden("f1", t, 2, par)
                if not live(t - SHIFT):
                    norm("f1", t + 3)
                copy_attnT(t - 3)
                evacuate_x("at", t - 2, t, 1)
                hidden("f1", t, 3, par)
                evacuate_x("f2", t + 2 - SHIFT, t, 2)
                hidden("f2", t, 0, par)
                exp_logits("f2", t + 2 - SHIFT)
                if live(t - SHIFT):
                    norm("f1", t + 3)
                hidden("f2", t, 1, par)
                hidden("f2", t, 2, par)
                exp_q(t - 2)
                hidden("f2", t, 3, par)
                copy_v(t - 2)
                exp_k(t - 2)

            minus_one = c_mone
            pipeline(act, iteration)

        @block.gpsimd
        def _(pool):
            gp = nc.gpsimd
            gp.memset(router_sb[:], 0.0).then_inc(s_zero, 1)
            gp.memset(c_eps[:], EPS)
            gp.memset(c_mhalf[:], -0.5)
            gp.memset(c_mone[:], -1.0).then_inc(s_pconst, 1)
            pool.wait_ge(s_pconst, 1)

            def inv_std(s, n):
                if not live(n):
                    return
                pool.wait_ge(s_mv[s], value(n + 1))
                gp.tensor_tensor(ve[s][:], mv[s][:, :, 1], c_eps[:], ALU.add).then_inc(s_ve[s], 1)
                gp.tensor_tensor(nm[s][:], mv[s][:, :, 0], c_mone[:], ALU.mult).then_inc(s_ve[s], 1)
                pool.wait_ge(s_ve[s], value(n * 2 + 2))
                gp.tensor_tensor(rstd[s][:], ve[s][:], c_mhalf[:], ALU.pow).then_inc(s_rstd[s], 1)
                pool.wait_ge(s_rstd[s], value(n + 1))
                gp.tensor_tensor(nbias[s][:], nm[s][:], rstd[s][:], ALU.mult).then_inc(s_nb[s], 1)

            def low_part(s, n, par):
                if not live(n):
                    return
                u = par if nx[s] == 2 else 0
                pool.wait_ge(s_hi[s], value(n + 1))
                gp.tensor_tensor(x_lo[s][u][:], xT[s][:], x_hi[s][u][:].bitcast(F32), ALU.subtract).then_inc(s_lo[s], 1)

            def masked_comparison(s, n):
                if not live(n):
                    return
                pool.wait_ge(s_geq[s], value(n + 1))
                for k in range(TG):
                    i = gp.tensor_tensor(ahead[s][:, k, :, 0:EXP], geq[s][:, k, :, :], before, ALU.mult)
                i.then_inc(s_ahead[s], 1)

            def sum_experts(s, t, j):
                n = t - off[s]
                if not live(n):
                    return
                pool.wait_ge(s_prod[s], value(n * (2 * TG) + (2 * j + 2)))
                p = prod[j % 2]
                gp.tensor_tensor(t1[:], p[:, 0:4, :], p[:, 4:8, :], ALU.add).then_inc(s_t1[s], 1)
                pool.wait_ge(s_t1[s], value(n * TG + j + 1))
                gp.tensor_tensor(t2[:], t1[:, 0:2, :], t1[:, 2:4, :], ALU.add).then_inc(s_t2[s], 1)
                pool.wait_ge(s_t2[s], value(n * TG + j + 1))
                if due(n * TG + j):
                    pool.wait_ge(s_x[s], value(n * TG + j))
                if j == 0:
                    m = through(other[s], s, t) * TG
                    if due(m):
                        pool.wait_ge(s_x[other[s]], value(m))
                gp.tensor_tensor(t3[:], t2[:, 0, :], t2[:, 1, :], ALU.add).then_inc(s_t3[s], 1)
                pool.wait_ge(s_t3[s], value(n * TG + j + 1))
                tile = x_sb[:, bass.ds(value(n * TG + j), 1), :].rearrange("p a d -> p (a d)")
                gp.tensor_tensor(tile, t3[:], tile, ALU.add).then_inc(s_x[s], 1)

            def iteration(t, par):
                low_part("f1", t + 2, par)
                sum_experts("f1", t, 0)
                inv_std("f1", t + 3)
                masked_comparison("f1", t + 2)
                sum_experts("f1", t, 1)
                sum_experts("f1", t, 2)
                low_part("at", t - 2, 0)
                sum_experts("f1", t, 3)
                low_part("f2", t + 2 - SHIFT, (par + SHIFT) % 2)
                inv_std("at", t - 1)
                sum_experts("f2", t, 0)
                masked_comparison("f2", t + 2 - SHIFT)
                sum_experts("f2", t, 1)
                inv_std("f2", t + 3 - SHIFT)
                sum_experts("f2", t, 2)
                sum_experts("f2", t, 3)

            pipeline(pool, iteration)

        @block.vector
        def _(dve):
            v = nc.vector
            dve.wait_ge(s_w1, 16)
            v.tensor_copy(w1_hi[:], w1_raw).then_inc(s_w1hi, 1)
            dve.wait_ge(s_w1hi, 1)
            v.tensor_tensor(w1_lo[:], w1_raw, w1_hi[:].bitcast(F32), ALU.subtract).then_inc(s_w1lo, 1)
            v.memset(v_sb[:, :, D:D + 1], 1.0)
            dve.wait_ge(s_con, 16)
            for s in FFN:
                for k in range(TG):
                    i = v.tensor_copy(ahead[s][:, k, :, EXP], after)
            i.then_inc(s_set, 1)

            def split_attention_weights():
                dve.wait_ge(s_wqkv, 16)
                wq, wkv = wqkv_raw[:, 0:D], wqkv_raw[:, D:3 * D]
                h2 = D // 2
                v.tensor_copy(wq_hi[:, 0, :], wq)
                v.tensor_copy(wq_hi[:, 1, 0:h2], wq[:, h2:D])
                v.tensor_copy(wq_hi[:, 1, h2:D], wq[:, 0:h2])
                v.tensor_copy(wkv_hi[:], wkv).then_inc(s_wa_hi, 1)
                dve.wait_ge(s_wa_hi, 1)
                v.tensor_tensor(wq_lo[:, 0, :], wq, wq_hi[:, 0, :].bitcast(F32), ALU.subtract)
                v.tensor_tensor(wq_lo[:, 1, 0:h2], wq[:, h2:D], wq_hi[:, 1, 0:h2].bitcast(F32), ALU.subtract)
                v.tensor_tensor(wq_lo[:, 1, h2:D], wq[:, 0:h2], wq_hi[:, 1, h2:D].bitcast(F32), ALU.subtract)
                v.tensor_tensor(wkv_lo[:], wkv, wkv_hi[:].bitcast(F32), ALU.subtract).then_inc(s_wa_lo, 1)

            def stats(s, n, par):
                if not live(n):
                    return
                if s == "f1":
                    dve.wait_ge(s_load[par], value(n * 8 + (16 - 8 * par)))
                elif s == "at":
                    dve.wait_ge(s_x["f1"], value(n * TG + TG))
                else:
                    dve.wait_ge(A["x2"], value(n + 1))
                if due(n):
                    dve.wait_ge(s_nb[s], value(n))
                dve.sem_inc(s_gate, 1)
                for k in range(TG):
                    tile = x_sb[:, bass.ds(value(n * TG + k), 1), :].rearrange("p a d -> p (a d)")
                    i = v.bn_stats(bn[s][:, k, :], tile)
                i.then_inc(s_bn[s], 1)
                dve.wait_ge(s_bn[s], value(n + 1))
                dve.sem_inc(s_gate, 1)
                for k in range(TG):
                    i = v.bn_aggr(mv[s][:, k, :], bn[s][:, k, :])
                i.then_inc(s_mv[s], 1)

            def high_part(s, n, par):
                if not live(n):
                    return
                u = par if nx[s] == 2 else 0
                dve.wait_ge(s_xT[s], value(n + 1))
                v.tensor_copy(x_hi[s][u][:], xT[s][:]).then_inc(s_hi[s], 1)

            def probabilities(s, n):
                if not live(n):
                    return
                dve.wait_ge(s_ex[s], value(n + 1))
                v.tensor_scalar(r1[s][:], ex[s][:], 1.0, None, ALU.add).then_inc(s_rt[s], 1)
                dve.wait_ge(s_rt[s], value(n * RSTEPS + 1))
                v.reciprocal(prob[s][:], r1[s][:]).then_inc(s_rt[s], 1)
                dve.wait_ge(s_rt[s], value(n * RSTEPS + 2))
                for k in range(TG):
                    i = v.tensor_tensor(geq[s][:, k, :, :], prob[s][:, k, :].unsqueeze(1).to_broadcast([P, EXP, EXP]),
                                        prob[s][:, k, :].unsqueeze(2).to_broadcast([P, EXP, EXP]), ALU.is_ge)
                i.then_inc(s_geq[s], 1)

            def top_two(s, n):
                if not live(n):
                    return
                dve.wait_ge(s_ahead[s], value(n + 1))
                v.reduce_sum(r1[s][:], ahead[s][:], axis=AX.X).then_inc(s_rt[s], 1)
                for k in range(TG):
                    i = v.reduce_sum(r2[s][:, k, :], ahead[s][:, k, :, 0:EXP].rearrange("p a b -> p b a"), axis=AX.X)
                i.then_inc(s_rt[s], 1)
                dve.wait_ge(s_rt[s], value(n * RSTEPS + 4))
                v.tensor_tensor(r1[s][:], r1[s][:], r2[s][:], ALU.subtract).then_inc(s_rt[s], 1)
                dve.wait_ge(s_rt[s], value(n * RSTEPS + 5))
                v.scalar_tensor_tensor(chosen[s][:], r1[s][:], float(TOPK), prob[s][:], ALU.is_lt, ALU.mult) \
                    .then_inc(s_rt[s], 1)
                dve.wait_ge(s_rt[s], value(n * RSTEPS + 6))
                v.reduce_sum(tot[s][:], chosen[s][:], axis=AX.X).then_inc(s_rt[s], 1)
                dve.wait_ge(s_rt[s], value(n * RSTEPS + 7))
                v.tensor_scalar(tot[s][:], tot[s][:], 1e-20, 2.0, ALU.add, ALU.mult).then_inc(s_rt[s], 1)

            def expert_weights(s, n, par):
                if not live(n):
                    return
                dve.wait_ge(s_rt[s], value(n * RSTEPS + 8))
                v.reciprocal(r2[s][:, :, 0], tot[s][:]).then_inc(s_cw[s], 1)
                dve.wait_ge(s_cw[s], value(n * 2 + 1))
                v.tensor_tensor(cw[s][par][:], chosen[s][:], r2[s][:, :, 0:1].to_broadcast([P, TG, EXP]), ALU.mult) \
                    .then_inc(s_cw[s], 1)

            def weigh(s, t, j, half, par):
                n = t - off[s]
                if not live(n):
                    return
                dve.wait_ge(s_p2[s], value(n * (2 * TG) + (2 * j + half + 1)))
                if j == 0 and half == 0:
                    dve.wait_ge(s_cw[s], value(n * 2 + 2))
                if half == 0:
                    if due(n * TG + (j - 1)):
                        dve.wait_ge(s_t1[s], value(n * TG + (j - 1)))
                    if j < 2:
                        m = through(other[s], s, t) * TG + (j - 1)
                        if due(m):
                            dve.wait_ge(s_t1[other[s]], value(m))
                u = (par + off[s]) % 2
                e = slice(half * EH, (half + 1) * EH)
                v.tensor_tensor(prod[j % 2][:, e, :], yp[half][:].rearrange("p (e d) -> p e d", e=EH),
                                cw[s][u][:, j, e].unsqueeze(2).to_broadcast([P, EH, D]), ALU.mult).then_inc(s_prod[s], 1)

            def rope_q_cos(n):
                if live(n):
                    dve.wait_ge(A["q"], value(n + 1))
                    if due(n):
                        dve.wait_ge(A["qf"], value(n))
                    v.tensor_tensor(qa[:], a0[:].rearrange("p (b t) -> p b t", b=BG), cos_q, ALU.mult).then_inc(A["qa"], 1)

            def rope_q_sin(n):
                if not live(n):
                    return
                dve.wait_ge(A["qr"], value(n + 1))
                v.tensor_tensor(qb[:], a1[:].rearrange("p (b t) -> p b t", b=BG), sin_q, ALU.mult).then_inc(A["qb"], 1)
                dve.wait_ge(A["qb"], value(n + 1))
                v.scalar_tensor_tensor(qa[:], qa[:], 1.0, qb[:], ALU.add, ALU.add).then_inc(A["xq"], 1)

            def q_features(n):
                if live(n):
                    dve.wait_ge(A["eq"], value(n + 1))
                    if due(n):
                        dve.wait_ge(A["nd"], value(n))
                    v.scalar_tensor_tensor(qf[:].rearrange("p (b t) -> p b t", b=BG), eq[:], 1.0, qa[:], ALU.min, ALU.max) \
                        .then_inc(A["qf"], 1)

            def rope_k(n, b):
                if not live(n):
                    return
                dve.wait_ge(A["kv"], value(n * BG + b + 1))
                if b == 0:
                    if due(n):
                        dve.wait_ge(A["kf"], value(n))
                k = (a2, a0)[b][:].rearrange("p (r c) -> p r c", r=RT)[:, :, 0:D]
                tiles = slice(b * RT, (b + 1) * RT)
                v.tensor_tensor(ka[:, tiles, :], k, cos_k, ALU.mult).then_inc(A["ka"], 1)
                swapped = k.rearrange("p r (w c) -> p r w c", w=2)[:, :, ::-1, :]
                v.tensor_tensor(kb[:, tiles, :].rearrange("p r (w c) -> p r w c", w=2), swapped,
                                sin_k.rearrange("p r (w c) -> p r w c", w=2), ALU.mult).then_inc(A["kb"], 1)
                if b == BG - 1:
                    dve.wait_ge(A["kb"], value(n * BG + BG))
                    v.scalar_tensor_tensor(ka[:], ka[:], 1.0, kb[:], ALU.add, ALU.add).then_inc(A["xk"], 1)

            def k_features(n):
                if live(n):
                    dve.wait_ge(A["ek"], value(n + 1))
                    v.scalar_tensor_tensor(kf[:], ek[:], 1.0, ka[:], ALU.min, ALU.max).then_inc(A["kf"], 1)

            def mask_state(n):
                if not live(n):
                    return
                dve.wait_ge(A["state"], value(n + 1))
                st = a1[:].rearrange("p (b c) -> p b c", b=BG)
                v.tensor_tensor(kvm[:, :, 0:D], st[:, :, 0:D], same_head, ALU.mult).then_inc(A["kvm"], 1)
                v.tensor_tensor(kvm[:, :, D:KVW], st[:, :, D:D + 1].to_broadcast([P, BG, HEADS]), in_head, ALU.mult) \
                    .then_inc(A["kvs"], 1)

            def normalise(n):
                if not live(n):
                    return
                dve.wait_ge(A["nd"], value(n + 1))
                for b in range(BG):
                    nd = (a2, a0)[b][:].rearrange("p (r c) -> p r c", r=RT)
                    i = v.tensor_scalar(den[:, b * RT:(b + 1) * RT, :], nd[:, :, D:KVW], 1e-6, None, ALU.max)
                i.then_inc(A["den"], 1)
                dve.wait_ge(A["den"], value(n + 1))
                v.reciprocal(rden[:], den[:]).then_inc(A["rden"], 1)
                dve.wait_ge(A["rden"], value(n + 1))
                for b in range(BG):
                    nd = (a2, a0)[b][:].rearrange("p (r c) -> p r c", r=RT)
                    i = v.tensor_tensor(attn[:, b * RT:(b + 1) * RT, :].rearrange("p r (h c) -> p r h c", h=HEADS),
                                        nd[:, :, 0:D].rearrange("p r (h c) -> p r h c", h=HEADS),
                                        rden[:, b * RT:(b + 1) * RT, :].unsqueeze(3).to_broadcast([P, RT, HEADS, HD]),
                                        ALU.mult)
                i.then_inc(A["attn"], 1)

            def add_attention(n):
                if live(n):
                    dve.wait_ge(A["y"], value(n + 1))
                    tiles = x_sb[:, bass.ds(value(n * TG), TG), :]
                    v.tensor_tensor(tiles, a2[:].rearrange("p (k d) -> p k d", k=TG), tiles, ALU.add).then_inc(A["x2"], 1)

            def iteration(t, par):
                p2 = (par + SHIFT) % 2
                if first_time(True, t):
                    split_attention_weights()
                k_features(t - 3)
                high_part("f1", t + 2, par)
                weigh("f1", t, 0, 0, par)
                weigh("f1", t, 0, 1, par)
                stats("f1", t + 3, (par + 1) % 2)
                mask_state(t - 3)
                probabilities("f1", t + 2)
                weigh("f1", t, 1, 0, par)
                weigh("f1", t, 1, 1, par)
                top_two("f1", t + 2)
                weigh("f1", t, 2, 0, par)
                normalise(t - 3)
                weigh("f1", t, 2, 1, par)
                high_part("at", t - 2, 0)
                weigh("f1", t, 3, 0, par)
                weigh("f1", t, 3, 1, par)
                expert_weights("f1", t + 2, par)
                add_attention(t - 3)
                high_part("f2", t + 2 - SHIFT, p2)
                stats("at", t - 1, 0)
                weigh("f2", t, 0, 0, par)
                weigh("f2", t, 0, 1, par)
                rope_q_cos(t - 2)
                probabilities("f2", t + 2 - SHIFT)
                weigh("f2", t, 1, 0, par)
                stats("f2", t + 3 - SHIFT, 0)
                weigh("f2", t, 1, 1, par)
                rope_q_sin(t - 2)
                top_two("f2", t + 2 - SHIFT)
                weigh("f2", t, 2, 0, par)
                weigh("f2", t, 2, 1, par)
                rope_k(t - 2, 0)
                rope_k(t - 2, 1)
                weigh("f2", t, 3, 0, par)
                q_features(t - 2)
                weigh("f2", t, 3, 1, par)
                expert_weights("f2", t + 2 - SHIFT, p2)

            pipeline(dve, iteration)


_INS = ["x", "wqkv", "wout", "router", "w1", "w2", "const"]


def kernel(L0_attn_x, L0_attn_W_qkv, L0_attn_W_out, L0_ffn_router_w, L0_ffn_w1, L0_ffn_w2):
    import concourse.bacc as bacc
    from concourse.bass_utils import run_bass_kernel_spmd

    w = np.asarray(L0_attn_W_qkv).reshape(D, 3, HEADS, 2, HALF)
    qk = w[:, 0:2].transpose(0, 1, 3, 2, 4).reshape(D, 2 * D)
    arrays = {
        "x": np.ascontiguousarray(L0_attn_x),
        "wqkv": np.ascontiguousarray(np.concatenate([qk, w[:, 2].reshape(D, D)], 1)),
        "wout": np.ascontiguousarray(L0_attn_W_out),
        "router": np.ascontiguousarray(np.asarray(L0_ffn_router_w).T),
        "w1": np.ascontiguousarray(L0_ffn_w1),
        "w2": np.ascontiguousarray(L0_ffn_w2),
        "const": CONST,
    }
    nc = bacc.Bacc("TRN2", target_bir_lowering=False, num_devices=1,
                   dynamic_dma_scratch_size=1024)
    aps = [nc.dram_tensor(f"in_{n}", arrays[n].shape, F32, kind="ExternalInput").ap() for n in _INS]
    out = nc.dram_tensor("out_x", (B, T, D), F32, kind="ExternalOutput").ap()
    build(nc, *aps, out)
    r = run_bass_kernel_spmd(nc, [{f"in_{n}": arrays[n] for n in _INS}], core_ids=[0])
    return r.results[0]["out_x"]
```

```python
from contextlib import ExitStack

import numpy as np

import concourse.bass as bass
from concourse import mybir

F32 = mybir.dt.float32
F32R = mybir.dt.float32r
ALU = mybir.AluOpType
ACT = mybir.ActivationFunctionType
AX = mybir.AxisListType

B, T, D = 32, 256, 128
P = 128
RT = T // P
BG = 2
TG = BG * RT
NTOK = TG * P
NG = B // BG
NT = B * RT
HEADS, HD = 16, 8
HALF = HD // 2
WIDTHS = [128] * 4 + [256] * 4
EXP = len(WIDTHS)
WTOT = sum(WIDTHS)
NC = WTOT // P
CQ = NC // TG
STAGE = NC // 2
PLACES = 2 * NC
DOWN_BEHIND = 9
EXPERT = [e for e, w_ in enumerate(WIDTHS) for _ in range(w_ // P)]
TOPK = 2
PAD = 96
EH = EXPERT[NC // 2]
TINY = 1.2e-38
KVW = D + HEADS
ROPE_BASE = 500000.0
EPS = 1e-5
SHIFT = 5
T_FIRST, T_LAST = -3, NG + SHIFT


class Step:

    def __init__(self, i, a, c, trips):
        self.i, self.a, self.c, self.trips = i, a, c, trips

    def __add__(self, k):
        return Step(self.i, self.a, self.c + k, self.trips)

    def __sub__(self, k):
        return self + (-k)

    def __mul__(self, k):
        return Step(self.i, self.a * k, self.c * k, self.trips)

    @property
    def last(self):
        return self.c + self.a * (self.trips - 1)

    @property
    def value(self):
        return self.i * self.a + self.c


def first(v):
    return v.c if isinstance(v, Step) else v


def last(v):
    return v.last if isinstance(v, Step) else v


def value(v):
    return v.value if isinstance(v, Step) else v


def due(v):
    assert (first(v) > 0) == (last(v) > 0)
    return first(v) > 0


def live(n):
    return first(n) >= 0 and last(n) < NG


def first_time(stream, n):
    return stream and not isinstance(n, Step) and n == 0


def done(n):
    if last(n) <= 0:
        return 0
    if first(n) >= NG:
        return NG
    assert first(n) >= 0 and last(n) <= NG
    return n


def stages(t):
    ns = [t + 3, t + 2, t + 1, t, t - 1, t - 2]
    ns += [t + 3 - SHIFT, t + 2 - SHIFT, t + 1 - SHIFT, t - SHIFT]
    return tuple((n >= 0) + (n > 0) + (n >= NG) for n in ns)


def runs():
    out = []
    for t in range(T_FIRST, T_LAST + 1, 2):
        kind = (stages(t), stages(t + 1))
        if out and out[-1][2] == kind and kind[0] == kind[1]:
            out[-1][1] += 1
        else:
            out.append([t, 1, kind])
    return [(t, trips) for t, trips, _ in out]


def pipeline(eng, iteration):
    for t0, trips in runs():
        if trips == 1:
            for u in range(2):
                iteration(t0 + u, (t0 + u) % 2)
        else:
            with eng.Fori(0, trips) as i:
                for u in range(2):
                    iteration(Step(i, 2, t0 + u, trips), (t0 + u) % 2)


def constant_columns():
    inv = (1.0 / ROPE_BASE ** (np.arange(0, HD, 2, dtype=np.float32) / np.float32(HD))).astype(np.float32)
    ang = np.arange(T, dtype=np.float32)[:, None] * inv[None, :]
    cos, sin = np.cos(ang).astype(np.float32), np.sin(ang).astype(np.float32)
    col_f = np.arange(D) % HALF
    sign = np.where(np.arange(D) < D // 2, -1.0, 1.0).astype(np.float32)
    cos_k, sin_k = cos[:, col_f], sin[:, col_f] * sign
    scale = np.float32(HD ** -0.5)
    tok = (RT * np.arange(P)[None, :] + np.arange(RT)[:, None]).ravel()
    head_qk = (np.arange(D) % (D // 2)) // HALF
    head_v = np.arange(D) // HD
    a, b = np.arange(EXP)[:, None], np.arange(EXP)[None, :]
    parts = {
        "ident": np.eye(P),
        "cos_q": cos_k[tok].T * scale,
        "sin_q": sin_k[tok].T * scale,
        "cos_k": cos_k.reshape(P, RT * D),
        "sin_k": sin_k.reshape(P, RT * D),
        "same_head": head_qk[:, None] == head_v[None, :],
        "in_head": head_qk[:, None] == np.arange(HEADS)[None, :],
        "before": np.broadcast_to((b < a).reshape(1, EXP * EXP), (P, EXP * EXP)),
        "after": np.broadcast_to(EXP - 1 - np.arange(EXP)[None, :], (P, EXP)),
    }
    where, at = {}, 0
    for name, v in parts.items():
        where[name] = (at, at + v.shape[1])
        at += v.shape[1]
    return np.concatenate([np.asarray(v, np.float32) for v in parts.values()], 1), where


CONST, WHERE = constant_columns()


def build(nc, x_in, wqkv, wout, router, w1, w2, const, out, rows):
    ctx = ExitStack()
    with ctx:
        def sb(name, shape, dt=F32):
            return ctx.enter_context(nc.sbuf_tensor(name, shape, dt))

        def sem(name):
            return ctx.enter_context(nc.semaphore(name))

        FFN = ("f1", "f2")
        STREAMS = ("f1", "at", "f2")

        x_sb = sb("x_sb", [P, NT, D])
        con = sb("con", [P, CONST.shape[1]])
        w1_hi = sb("w1_hi", [P, WTOT], F32R)
        w1_lo = sb("w1_lo", [P, WTOT], F32R)
        w2_hi = sb("w2_hi", [P, NC, D], F32R)
        w2_lo = sb("w2_lo", [P, NC, D], F32R)
        router_sb = sb("router_sb", [P, PAD])
        wq_hi, wq_lo = sb("wq_hi", [P, 2, D], F32R), sb("wq_lo", [P, 2, D], F32R)
        wkv_hi, wkv_lo = sb("wkv_hi", [P, 2 * D], F32R), sb("wkv_lo", [P, 2 * D], F32R)
        wout_sb = sb("wout_sb", [P, D])
        hid = sb("hid", [P, STAGE, NTOK])
        h_hi = sb("h_hi", [P, NC, NTOK], F32R)
        h_lo = sb("h_lo", [P, NC, NTOK], F32R)
        g_tok = {s: sb(f"g_tok_{s}", [P, EXP, TG]) for s in FFN}
        g_row = {s: sb(f"g_row_{s}", [EXP * TG, P]) for s in FFN}
        g_all = {s: sb(f"g_all_{s}", [P, EXP, NTOK]) for s in FFN}
        early = g_all["f2"][:].rearrange("p e t -> p (e t)")
        w1_raw, w2_raw = early[:, 0:WTOT], early[:, WTOT:2 * WTOT]
        wqkv_raw = early[:, 2 * WTOT:2 * WTOT + 3 * D]
        xn = {s: sb(f"xn_{s}", [P, TG, D]) for s in STREAMS}
        xT = sb("xT", [P, NTOK])
        xT = {s: xT for s in STREAMS}
        nx = {"f1": 2, "at": 1, "f2": 2}
        x_hi = {s: [sb(f"x_hi_{s}{u}", [P, NTOK], F32R) for u in range(nx[s])] for s in STREAMS}
        x_lo = {s: [sb(f"x_lo_{s}{u}", [P, NTOK], F32R) for u in range(nx[s])] for s in STREAMS}
        bn = {s: sb(f"bn_{s}", [P, TG, 6]) for s in STREAMS}
        mv = {s: sb(f"mv_{s}", [P, TG, 2]) for s in STREAMS}
        ve = {s: sb(f"ve_{s}", [P, TG]) for s in STREAMS}
        nm = {s: sb(f"nm_{s}", [P, TG]) for s in STREAMS}
        rstd = {s: sb(f"rstd_{s}", [P, TG]) for s in STREAMS}
        nbias = {s: sb(f"nbias_{s}", [P, TG]) for s in STREAMS}
        c_eps, c_mhalf, c_mone = sb("c_eps", [P, TG]), sb("c_mhalf", [P, TG]), sb("c_mone", [P, TG])
        ex = {s: sb(f"ex_{s}", [P, TG, EXP]) for s in FFN}
        prob = {s: sb(f"prob_{s}", [P, TG, EXP]) for s in FFN}
        geq = {s: sb(f"geq_{s}", [P, TG, EXP, EXP]) for s in FFN}
        ahead = {s: sb(f"ahead_{s}", [P, TG, EXP, EXP + 1]) for s in FFN}
        r1 = {s: sb(f"r1_{s}", [P, TG, EXP]) for s in FFN}
        r2 = {s: sb(f"r2_{s}", [P, TG, EXP]) for s in FFN}
        pick = {s: sb(f"pick_{s}", [P, TOPK, TG, EXP]) for s in FFN}
        p_top = {s: sb(f"p_top_{s}", [P, TOPK, TG]) for s in FFN}
        tot = {s: sb(f"tot_{s}", [P, TG]) for s in FFN}
        rtot = {s: sb(f"rtot_{s}", [P, TG]) for s in FFN}
        cw = {s: sb(f"cw_{s}", [P, TOPK, TG]) for s in FFN}
        cwt = {s: sb(f"cwt_{s}", [P, TOPK, TG]) for s in FFN}
        root = {s: sb(f"root_{s}", [P, TOPK, TG]) for s in FFN}
        g_top = {s: sb(f"g_top_{s}", [P, TOPK, TG]) for s in FFN}
        c_half = sb("c_half", [P, TOPK, TG])
        yT = sb("yT", [P, NTOK])
        qa, qb = sb("qa", [P, BG, T]), sb("qb", [P, BG, T])
        eq = qb
        qf = sb("qf", [P, NTOK])
        ka, kb = sb("ka", [P, TG, D]), sb("kb", [P, TG, D])
        ek = kb
        kf = sb("kf", [P, TG, D])
        v_sb = sb("v_sb", [P, TG, D + 1])
        kvm = sb("kvm", [P, BG, KVW])
        den = sb("den", [P, TG, HEADS])
        rden = sb("rden", [P, TG, HEADS])
        attn = sb("attn", [P, TG, D])
        attnT = attn[:].rearrange("p k d -> p (k d)")

        def cc(name):
            a, b = WHERE[name]
            return con[:, a:b]

        ident = cc("ident")
        cos_q = cc("cos_q").unsqueeze(1).to_broadcast([P, BG, T])
        sin_q = cc("sin_q").unsqueeze(1).to_broadcast([P, BG, T])
        cos_k = cc("cos_k").rearrange("p (r d) -> p r d", r=RT)
        sin_k = cc("sin_k").rearrange("p (r d) -> p r d", r=RT)
        same_head = cc("same_head").unsqueeze(1).to_broadcast([P, BG, D])
        in_head = cc("in_head").unsqueeze(1).to_broadcast([P, BG, HEADS])
        before = cc("before").rearrange("p (a b) -> p a b", a=EXP)
        after = cc("after")

        bank = [ctx.enter_context(nc.psum_tensor(f"bank{i}", [P, 512], F32)) for i in range(8)]
        tp = bank[0]
        hp = bank[1:3]
        yp = {"f1": bank[3], "f2": bank[4]}
        a0, a1, a2 = bank[5:8]

        s_load = [sem(f"s_load{u}") for u in range(2)]
        s_w1, s_w2, s_con, s_wqkv, s_router, s_wout = (
            sem(n) for n in ("s_w1", "s_w2", "s_con", "s_wqkv", "s_router", "s_wout"))
        s_store = sem("s_store")
        s_gate = sem("s_gate")
        s_gate_sp = sem("s_gate_sp")
        s_w1hi, s_w1lo, s_w2hi, s_w2lo, s_wa_hi, s_wa_lo = (
            sem(n) for n in ("s_w1hi", "s_w1lo", "s_w2hi", "s_w2lo", "s_wa_hi", "s_wa_lo"))
        s_zero, s_pconst, s_set = sem("s_zero"), sem("s_pconst"), sem("s_set")

        def per(name, keys):
            return {s: sem(f"s_{name}_{s}") for s in keys}

        s_bn = per("bn", STREAMS)
        s_mv = per("mv", STREAMS)
        s_ve = per("ve", STREAMS)
        s_rstd = per("rstd", STREAMS)
        s_nb = per("nb", STREAMS)
        s_xn = per("xn", STREAMS)
        s_t = per("t", STREAMS)
        s_xT = per("xT", STREAMS)
        s_hi = per("hi", STREAMS)
        s_lo = per("lo", STREAMS)
        s_logit = per("logit", FFN)
        s_ex = per("ex", FFN)
        s_rt = per("rt", FFN)
        s_geq = per("geq", FFN)
        s_ahead = per("ahead", FFN)
        s_cw = per("cw", FFN)
        s_root = per("root", FFN)
        s_gm = per("gm", FFN)
        s_gt = per("gt", FFN)
        s_ct = per("ct", FFN)
        s_gr = per("gr", FFN)
        s_gd = per("gd", FFN)
        s_ga = {s: [sem(f"s_ga_{s}{h}") for h in range(2)] for s in FFN}
        s_p1 = per("p1", FFN)
        s_z = per("z", FFN)
        s_sq = per("sq", FFN)
        s_hhi = per("hhi", FFN)
        s_hlo = per("hlo", FFN)
        s_p2 = per("p2", FFN)
        s_yT = per("yT", FFN)
        s_y = per("y", FFN)
        s_x = per("x", FFN)
        names = "q qr qa qb xq eq qf kv ka kb v xk ek kf state kvm kvs nd den rden attn at atT y x2".split()
        A = {n: sem(f"s_a_{n}") for n in names}
        RSTEPS = 9
        other = {"f1": "f2", "f2": "f1"}
        off = {"f1": 0, "f2": SHIFT}

        def turns(s, t):
            return done(t + 1 + (1 if s == "f2" else 0) - off[other[s]])

        def alone(s, t):
            return not live(t + 1 - SHIFT) if s == "f1" else not live(t + 2)

        def chunks(t, place, behind=0):
            out = []
            for s, start in (("f1", 0), ("f2", NC)):
                for back in range(2):
                    k = place + PLACES * back - start - behind
                    step = 2 if alone(s, t - back) else 1
                    n = t - back + 1 - off[s]
                    if live(n) and k % step == 0 and 0 <= k // step < NC:
                        out.append((s, n, k // step, back))
            return out

        x_dram = x_in.rearrange("b (p r) d -> p b (r d)", r=RT)
        o_dram = out.rearrange("b (p r) d -> p b (r d)", r=RT)
        x_rows = x_sb[:].rearrange("p (b r) d -> p b (r d)", r=RT)

        block = ctx.enter_context(nc.Block())

        @block.sync
        def _(sp):
            def load(n, u):
                g, before = value(n), value((n - u) * 8)
                if due((n - u) * 8):
                    sp.wait_ge(s_load[u], before)
                    sp.sem_inc(s_gate_sp, 1)
                sp.dma_start(x_rows[:, bass.ds(g * BG, BG), :], x_dram[:, bass.ds(g * BG, BG), :]) \
                    .then_inc(s_load[u], 16)

            def load_pairs(n, trips):
                with sp.Fori(0, trips) as i:
                    for u in range(2):
                        load(Step(i, 2, n + u, trips), u)

            def broadcast(s, n):
                if not live(n):
                    return
                made, read, written = value(n + 1), value(n * 16), value(n * 16 + 16)
                used = [value(n * NC - NC // 2), value(n * NC)]
                sp.wait_ge(s_gr[s], made)
                sp.sem_inc(s_gate_sp, 1)
                if due(n):
                    sp.wait_ge(s_ga[s][0], read)
                    sp.sem_inc(s_gate_sp, 1)
                    sp.wait_ge(s_ga[s][1], read)
                    sp.sem_inc(s_gate_sp, 1)
                sp.dma_start(rows[s].rearrange("e (k p) -> (e k) p", k=TG), g_row[s][:]).then_inc(s_gd[s], 16)
                sp.wait_ge(s_gd[s], written)
                sp.sem_inc(s_gate_sp, 1)
                if s == "f2" and not due(n):
                    sp.wait_ge(s_w1lo, 1)
                    sp.wait_ge(s_w2lo, 1)
                    sp.wait_ge(s_wa_lo, 1)
                for half, (e0, e1) in enumerate(((0, EH), (EH, EXP))):
                    if due(n):
                        sp.wait_ge(s_z[s], used[half])
                        sp.sem_inc(s_gate_sp, 1)
                    flat = rows[s][e0:e1].rearrange("e t -> (e t)").unsqueeze(0)
                    sp.dma_start(g_all[s][:, e0:e1, :].rearrange("p e t -> p (e t)"),
                                 flat.to_broadcast([P, (e1 - e0) * NTOK])).then_inc(s_ga[s][half], 16)

            def store(n):
                if not live(n):
                    return
                g, final = value(n), value(n + 1)
                sp.wait_ge(s_x["f2"], final)
                sp.sem_inc(s_gate_sp, 1)
                sp.dma_start(o_dram[:, bass.ds(g * BG, BG), :], x_rows[:, bass.ds(g * BG, BG), :]) \
                    .then_inc(s_store, 16)

            def iteration(t, par):
                broadcast("f2", t + 1 - SHIFT)
                broadcast("f1", t + 2)
                if first_time(True, t + 2):
                    load_pairs(4, 3)
                if first_time(True, t + 1):
                    load_pairs(10, NG // 2 - 5)
                if alone("f2", t - 2):
                    store(t - 1 - SHIFT)
                if not alone("f2", t - 1):
                    store(t - SHIFT)

            for n in range(4):
                load(n, n % 2)
            pipeline(sp, iteration)
            sp.wait_ge(s_store, NG * 16)

        @block.tensor
        def _(pe):
            mm = nc.tensor.matmul

            def tp_free(t, pos):
                n = [done(m + (pos > k)) for k, m in
                     enumerate((t + 2, t + 1 - SHIFT, t - 1, t + 2 - SHIFT, t + 2))]
                if due(n[0]):
                    pe.wait_ge(s_ex["f1"], value(n[0]))
                if due(n[1]):
                    pe.wait_ge(s_gr["f2"], value(n[1]))
                if due(n[2]):
                    pe.wait_ge(s_xT["at"], value(n[2]))
                if due(n[3]):
                    pe.wait_ge(s_ex["f2"], value(n[3]))
                if due(n[4]):
                    pe.wait_ge(s_gr["f1"], value(n[4]))

            def transpose(s, n, t, pos):
                if not live(n):
                    return
                pe.wait_ge(s_xn[s], value(n + 1))
                tp_free(t, pos)
                for k in range(TG):
                    i = nc.tensor.transpose(tp[:, k * P:(k + 1) * P], xn[s][:, k, :], ident)
                i.then_inc(s_t[s], 1)

            def weight_rows(s, n, t, pos):
                if not live(n):
                    return
                pe.wait_ge(s_gt[s], value(n + 1))
                tp_free(t, pos)
                nc.tensor.transpose(tp[0:EXP * TG, 0:P], g_tok[s][:].rearrange("p e k -> p (e k)"), ident) \
                    .then_inc(s_ct[s], 1)

            def logits(s, n):
                if not live(n):
                    return
                pe.wait_ge(s_xT[s], value(n + 1))
                if first_time(s == "f1", n):
                    pe.wait_ge(s_router, 16)
                for k in range(TG):
                    i = mm(tp[:, k * P:k * P + PAD], xT[s][:, k * P:(k + 1) * P], router_sb[:], start=True, stop=True)
                i.then_inc(s_logit[s], 1)

            def up(s, n, c, t, par):
                u = (par + 1 + off[s]) % 2
                if c == 0:
                    pe.wait_ge(s_lo[s], value(n + 1))
                    if first_time(s == "f1", n):
                        pe.wait_ge(s_w1lo, 1)
                if c < 2:
                    m = turns(s, t) * NC
                    if due(m):
                        pe.wait_ge(s_z[other[s]], value(m))
                m = n * NC + max(c - 1, 0)
                if due(m):
                    pe.wait_ge(s_z[s], value(m))
                w = slice(c * P, (c + 1) * P)
                o = hp[c % 2][:]
                mm(o, w1_hi[:, w], x_hi[s][u][:], start=True, stop=False)
                mm(o, w1_hi[:, w], x_lo[s][u][:], start=False, stop=False)
                mm(o, w1_lo[:, w], x_hi[s][u][:], start=False, stop=True).then_inc(s_p1[s], 1)

            def down(s, n, c, t0):
                pe.wait_ge(s_hlo[s], value(n * NC + c + 1))
                if c == 0:
                    if due(n):
                        if alone(s, t0 - 1):
                            pe.wait_ge(s_yT[s], value(n))
                        else:
                            pe.wait_ge(s_x[s], value(n))
                    if s == "f2" and not due(n):
                        pe.wait_ge(s_x["f1"], SHIFT)
                    if first_time(s == "f1", n):
                        pe.wait_ge(s_w2lo, 1)
                o = yp[s][:]
                mm(o, w2_hi[:, c, :], h_hi[:, c, :], start=(c == 0), stop=False)
                mm(o, w2_hi[:, c, :], h_lo[:, c, :], start=False, stop=False)
                i = mm(o, w2_lo[:, c, :], h_hi[:, c, :], start=False, stop=(c == NC - 1))
                if c % CQ == CQ - 1:
                    i.then_inc(s_p2[s], 1)

            def back(s, n, t0):
                if not live(n):
                    return
                pe.wait_ge(s_yT[s], value(n + 1))
                o = yp[s]
                if alone(s, t0):
                    o = yp[other[s]]
                    if due(n):
                        pe.wait_ge(s_x[s], value(n))
                    if s == "f2":
                        pe.wait_ge(s_x["f1"], NG)
                for k in range(TG):
                    i = nc.tensor.transpose(o[:, k * D:(k + 1) * D], yT[:, k * P:(k + 1) * P], ident)
                i.then_inc(s_y[s], 1)

            def quarter(t, j, par):
                for place in range(CQ * j, CQ * (j + 1)):
                    for s, n, c, ago in chunks(t, place):
                        up(s, n, c, t - ago, (par + ago) % 2)
                    for s, n, c, ago in chunks(t, place, DOWN_BEHIND):
                        down(s, n, c, t - ago)

            def split_product(o, parts):
                for k, (a, b) in enumerate(parts):
                    i = mm(o, a, b, start=(k == 0), stop=(k == len(parts) - 1))
                return i

            def q_proj(n, rot, o):
                hi, lo = x_hi["at"][0][:], x_lo["at"][0][:]
                return split_product(o, [(wq_hi[:, rot, :], hi), (wq_hi[:, rot, :], lo), (wq_lo[:, rot, :], hi)])

            def q(n):
                if not live(n):
                    return
                pe.wait_ge(s_lo["at"], value(n + 1))
                if first_time(True, n):
                    pe.wait_ge(s_wa_lo, 1)
                if due(n):
                    pe.wait_ge(A["attn"], value(n))
                q_proj(n, 0, a0[:]).then_inc(A["q"], 1)

            def q_rotated(n):
                if not live(n):
                    return
                if due(n):
                    pe.wait_ge(A["atT"], value(n))
                q_proj(n, 1, a1[:]).then_inc(A["qr"], 1)

            def kv(n, b):
                if not live(n):
                    return
                if b == 0:
                    if due(n):
                        pe.wait_ge(A["x2"], value(n))
                else:
                    pe.wait_ge(A["qa"], value(n + 1))
                for r in range(RT):
                    c = slice((b * RT + r) * P, (b * RT + r + 1) * P)
                    hi, lo = x_hi["at"][0][:, c], x_lo["at"][0][:, c]
                    i = split_product((a2, a0)[b][:, r * 2 * D:(r + 1) * 2 * D],
                                      [(hi, wkv_hi[:]), (lo, wkv_hi[:]), (hi, wkv_lo[:])])
                i.then_inc(A["kv"], 1)

            def state(n):
                if not live(n):
                    return
                pe.wait_ge(A["kf"], value(n + 1))
                if first_time(True, n):
                    pe.wait_ge(s_set, 1)
                pe.wait_ge(A["v"], value(n * BG + BG))
                for b in range(BG):
                    for r in range(RT):
                        k = b * RT + r
                        i = mm(a1[:, b * 2 * D:b * 2 * D + D + 1], kf[:, k, :], v_sb[:, k, :],
                               start=(r == 0), stop=(r == RT - 1))
                i.then_inc(A["state"], 1)

            def attend(n):
                if not live(n):
                    return
                pe.wait_ge(A["qf"], value(n + 1))
                pe.wait_ge(A["kvs"], value(n + 1))
                for b in range(BG):
                    for r in range(RT):
                        k = b * RT + r
                        i = mm((a2, a0)[b][:, r * 2 * D:r * 2 * D + KVW], qf[:, k * P:(k + 1) * P],
                               kvm[:, b, :], start=True, stop=True)
                i.then_inc(A["nd"], 1)

            def attn_transpose(n):
                if not live(n):
                    return
                pe.wait_ge(A["attn"], value(n + 1))
                for k in range(TG):
                    i = nc.tensor.transpose(a1[:, k * P:(k + 1) * P], attn[:, k, :], ident)
                i.then_inc(A["at"], 1)

            def out_proj(n):
                if not live(n):
                    return
                pe.wait_ge(A["atT"], value(n + 1))
                if first_time(True, n):
                    pe.wait_ge(s_wout, 16)
                for k in range(TG):
                    i = mm(a2[:, k * D:(k + 1) * D], attnT[:, k * P:(k + 1) * P], wout_sb[:], start=True, stop=True)
                i.then_inc(A["y"], 1)

            pe.wait_ge(s_con, 16)

            def iteration(t, par):
                transpose("f1", t + 2, t, 0)
                quarter(t, 0, par)
                state(t - 2)
                logits("f1", t + 2)
                quarter(t, 1, par)
                weight_rows("f2", t + 1 - SHIFT, t, 1)
                attend(t - 2)
                quarter(t, 2, par)
                transpose("at", t - 1, t, 2)
                quarter(t, 3, par)
                attn_transpose(t - 2)
                if alone("f1", t - 1):
                    back("f1", t, t - 1)
                if not alone("f2", t - 1):
                    back("f2", t - SHIFT, t - 1)
                transpose("f2", t + 2 - SHIFT, t, 3)
                quarter(t, 4, par)
                out_proj(t - 2)
                q(t - 1)
                logits("f2", t + 2 - SHIFT)
                quarter(t, 5, par)
                q_rotated(t - 1)
                weight_rows("f1", t + 2, t, 4)
                quarter(t, 6, par)
                kv(t - 1, 0)
                kv(t - 1, 1)
                quarter(t, 7, par)
                if alone("f2", t - 1):
                    back("f2", t - SHIFT, t - 1)
                if not alone("f1", t):
                    back("f1", t + 1, t)

            pipeline(pe, iteration)

        @block.scalar
        def _(act):
            fn = nc.scalar.activation
            act.dma_start(w1_raw, w1).then_inc(s_w1, 16)
            act.dma_start(con[:], const).then_inc(s_con, 16)
            act.wait_ge(s_zero, 1)
            act.dma_start(router_sb[:, 0:EXP], router).then_inc(s_router, 16)
            act.dma_start(w2_raw.rearrange("p (c d) -> p c d", c=NC), w2.rearrange("(c p) d -> p c d", p=P)) \
                .then_inc(s_w2, 16)
            act.dma_start(wqkv_raw, wqkv).then_inc(s_wqkv, 16)
            act.dma_start(wout_sb[:], wout).then_inc(s_wout, 16)
            act.wait_ge(s_w1, 16)
            fn(w1_hi[:], w1_raw, ACT.Copy).then_inc(s_w1hi, 1)

            def norm(s, n):
                if not live(n):
                    return
                act.wait_ge(s_nb[s], value(n + 1))
                if due(n):
                    act.wait_ge(s_t[s], value(n))
                for k in range(TG):
                    tile = x_sb[:, bass.ds(value(n * TG + k), 1), :].rearrange("p a d -> p (a d)")
                    i = fn(xn[s][:, k, :], tile, ACT.Identity, bias=nbias[s][:, k:k + 1], scale=rstd[s][:, k:k + 1])
                i.then_inc(s_xn[s], 1)

            def evacuate_x(s, n, t, pos):
                if not live(n):
                    return
                act.wait_ge(s_t[s], value(n + 1))
                for q, m in (("f1", t + 2), ("at", t - 1), ("f2", t + 2 - SHIFT)):
                    m = done(m + 1 if STREAMS.index(q) < pos else m)
                    if due(m):
                        act.wait_ge(s_lo[q], value(m))
                fn(xT[s][:], tp[:], ACT.Copy).then_inc(s_xT[s], 1)

            def exp_logits(s, n):
                if not live(n):
                    return
                act.wait_ge(s_logit[s], value(n + 1))
                if due(n * RSTEPS):
                    act.wait_ge(s_rt[s], value(n * RSTEPS))
                l = tp[:].rearrange("p (k e) -> p k e", k=TG)[:, :, 0:EXP]
                fn(ex[s][:], l, ACT.Exp, scale=-1.0).then_inc(s_ex[s], 1)

            def rows_of_weights(s, n):
                if not live(n):
                    return
                act.wait_ge(s_ct[s], value(n + 1))
                if due(n):
                    act.wait_ge(s_gd[s], value(n * 16))
                fn(g_row[s][:], tp[0:EXP * TG, 0:P], ACT.Copy).then_inc(s_gr[s], 1)

            def squares(t, j):
                todo = [k for place in range(CQ * j, CQ * (j + 1)) for k in chunks(t, place)]
                for k in range(len(todo) + 1):
                    if k < len(todo):
                        s, n, c, ago = todo[k]
                        h = hid[:, c % STAGE, :]
                        act.wait_ge(s_z[s], value(n * NC + c + 1))
                        fn(h, h, ACT.Square).then_inc(s_sq[s], 1)
                    if k > 0:
                        s, n, c, ago = todo[k - 1]
                        if c % CQ == 0 or k == 1:
                            m = turns(s, t - ago) * TG + (c // CQ + 1 - TG)
                            if due(m):
                                act.wait_ge(s_p2[other[s]], value(m))
                            m = n * TG + (c // CQ + 1 - TG)
                            if due(m):
                                act.wait_ge(s_p2[s], value(m))
                        act.wait_ge(s_sq[s], value(n * NC + c + 1))
                        fn(h_hi[:, c, :], hid[:, c % STAGE, :], ACT.Copy).then_inc(s_hhi[s], 1)

            def copy_yT(s, n, t):
                if not live(n):
                    return
                act.wait_ge(s_p2[s], value(n * TG + TG))
                if due(n):
                    act.wait_ge(s_y[s], value(n))
                m = done(t - SHIFT + 1) if s == "f1" else done(t + 1)
                if due(m):
                    act.wait_ge(s_y[other[s]], value(m))
                fn(yT[:], yp[s][:], ACT.Copy).then_inc(s_yT[s], 1)

            def exp_q(n):
                if live(n):
                    act.wait_ge(A["xq"], value(n + 1))
                    fn(eq[:], qa[:], ACT.Exp, bias=minus_one[:, 0:1]).then_inc(A["eq"], 1)

            def exp_k(n):
                if live(n):
                    act.wait_ge(A["xk"], value(n + 1))
                    fn(ek[:], ka[:], ACT.Exp, bias=minus_one[:, 0:1]).then_inc(A["ek"], 1)

            def copy_v(n):
                if not live(n):
                    return
                for b in range(BG):
                    act.wait_ge(A["kb"], value(n * BG + b + 1))
                    if b == 0:
                        if due(n):
                            act.wait_ge(A["state"], value(n))
                    src = (a2, a0)[b][:].rearrange("p (r c) -> p r c", r=RT)[:, :, D:2 * D]
                    fn(v_sb[:, b * RT:(b + 1) * RT, 0:D], src, ACT.Copy).then_inc(A["v"], 1)

            def copy_attnT(n):
                if live(n):
                    act.wait_ge(A["at"], value(n + 1))
                    fn(attnT, a1[:], ACT.Copy).then_inc(A["atT"], 1)

            act.wait_ge(s_pconst, 1)

            def iteration(t, par):
                n1, n2, n2_last = t + 1, t + 1 - SHIFT, t - SHIFT
                evacuate_x("f1", t + 2, t, 0)
                squares(t - 1, 7)
                if first_time(True, t + 2):
                    act.wait_ge(s_w2, 16)
                    fn(w2_hi[:], w2_raw.rearrange("p (c d) -> p c d", c=NC), ACT.Copy).then_inc(s_w2hi, 1)
                norm("at", t - 1)
                exp_logits("f1", t + 2)
                squares(t, 0)
                norm("f2", t + 2 - SHIFT)
                squares(t, 1)
                rows_of_weights("f2", n2)
                if not live(t - SHIFT):
                    norm("f1", t + 3)
                if alone("f1", t - 1):
                    copy_yT("f1", t, t - 1)
                evacuate_x("at", t - 1, t, 1)
                if not alone("f2", t - 1):
                    copy_yT("f2", n2_last, t)
                squares(t, 2)
                squares(t, 3)
                copy_attnT(t - 2)
                evacuate_x("f2", t + 2 - SHIFT, t, 2)
                if live(t - SHIFT):
                    norm("f1", t + 3)
                exp_logits("f2", t + 2 - SHIFT)
                squares(t, 4)
                squares(t, 5)
                rows_of_weights("f1", t + 2)
                if not alone("f1", t):
                    copy_yT("f1", n1, t)
                if alone("f2", t - 1):
                    copy_yT("f2", n2_last, t)
                squares(t, 6)
                exp_q(t - 1)
                copy_v(t - 1)
                exp_k(t - 1)

            minus_one = c_mone
            pipeline(act, iteration)

        @block.gpsimd
        def _(pool):
            gp = nc.gpsimd
            gp.memset(router_sb[:], 0.0).then_inc(s_zero, 1)
            gp.memset(c_eps[:], EPS)
            gp.memset(c_mhalf[:], -0.5)
            gp.memset(c_half[:], 0.5)
            gp.memset(c_mone[:], -1.0).then_inc(s_pconst, 1)
            pool.wait_ge(s_pconst, 1)

            def inv_std(s, n):
                if not live(n):
                    return
                pool.wait_ge(s_mv[s], value(n + 1))
                gp.tensor_tensor(ve[s][:], mv[s][:, :, 1], c_eps[:], ALU.add).then_inc(s_ve[s], 1)
                gp.tensor_tensor(nm[s][:], mv[s][:, :, 0], c_mone[:], ALU.mult).then_inc(s_ve[s], 1)
                pool.wait_ge(s_ve[s], value(n * 2 + 2))
                gp.tensor_tensor(rstd[s][:], ve[s][:], c_mhalf[:], ALU.pow).then_inc(s_rstd[s], 1)
                pool.wait_ge(s_rstd[s], value(n + 1))
                gp.tensor_tensor(nbias[s][:], nm[s][:], rstd[s][:], ALU.mult).then_inc(s_nb[s], 1)

            def low_part(s, n, par):
                if not live(n):
                    return
                u = par if nx[s] == 2 else 0
                pool.wait_ge(s_hi[s], value(n + 1))
                gp.tensor_tensor(x_lo[s][u][:], xT[s][:], x_hi[s][u][:].bitcast(F32), ALU.subtract).then_inc(s_lo[s], 1)

            def root_of_weights(s, n):
                if not live(n):
                    return
                pool.wait_ge(s_cw[s], value(n * 3 + 3))
                gp.tensor_tensor(root[s][:], cwt[s][:], c_half[:], ALU.pow).then_inc(s_root[s], 1)

            def remainders(t, *places):
                for place in places:
                    for s, n, c, _ in chunks(t, place):
                        pool.wait_ge(s_hhi[s], value(n * NC + c + 1))
                        gp.tensor_tensor(h_lo[:, c, :], hid[:, c % STAGE, :], h_hi[:, c, :].bitcast(F32),
                                         ALU.subtract).then_inc(s_hlo[s], 1)

            def iteration(t, par):
                remainders(t - 1, 21, 22)
                low_part("f1", t + 2, par)
                remainders(t - 1, 23)
                if first_time(True, t + 2):
                    pool.wait_ge(s_w2hi, 1)
                    gp.tensor_tensor(w2_lo[:], w2_raw.rearrange("p (c d) -> p c d", c=NC),
                                     w2_hi[:].bitcast(F32), ALU.subtract).then_inc(s_w2lo, 1)
                remainders(t, 0, 1)
                inv_std("f1", t + 3)
                remainders(t, 2, 3, 4, 5, 6, 7)
                low_part("at", t - 1, 0)
                remainders(t, 8)
                root_of_weights("f1", t + 2)
                remainders(t, 9, 10)
                low_part("f2", t + 2 - SHIFT, (par + SHIFT) % 2)
                remainders(t, 11)
                remainders(t, 12, 13, 14, 15)
                inv_std("at", t)
                remainders(t, 16, 17, 18, 19)
                inv_std("f2", t + 3 - SHIFT)
                remainders(t, 20)
                root_of_weights("f2", t + 2 - SHIFT)

            pipeline(pool, iteration)

        @block.vector
        def _(dve):
            v = nc.vector
            v.memset(v_sb[:, :, D:D + 1], 1.0)

            def set_ranks():
                dve.wait_ge(s_con, 16)
                for s in FFN:
                    for k in range(TG):
                        i = v.tensor_copy(ahead[s][:, k, :, EXP], after)
                i.then_inc(s_set, 1)

            def split_w1():
                dve.wait_ge(s_w1hi, 1)
                v.tensor_tensor(w1_lo[:], w1_raw, w1_hi[:].bitcast(F32), ALU.subtract).then_inc(s_w1lo, 1)

            def split_attention_weights():
                dve.wait_ge(s_wqkv, 16)
                wq, wkv = wqkv_raw[:, 0:D], wqkv_raw[:, D:3 * D]
                h2 = D // 2
                v.tensor_copy(wq_hi[:, 0, :], wq)
                v.tensor_copy(wq_hi[:, 1, 0:h2], wq[:, h2:D])
                v.tensor_copy(wq_hi[:, 1, h2:D], wq[:, 0:h2])
                v.tensor_copy(wkv_hi[:], wkv).then_inc(s_wa_hi, 1)
                dve.wait_ge(s_wa_hi, 1)
                v.tensor_tensor(wq_lo[:, 0, :], wq, wq_hi[:, 0, :].bitcast(F32), ALU.subtract)
                v.tensor_tensor(wq_lo[:, 1, 0:h2], wq[:, h2:D], wq_hi[:, 1, 0:h2].bitcast(F32), ALU.subtract)
                v.tensor_tensor(wq_lo[:, 1, h2:D], wq[:, 0:h2], wq_hi[:, 1, h2:D].bitcast(F32), ALU.subtract)
                v.tensor_tensor(wkv_lo[:], wkv, wkv_hi[:].bitcast(F32), ALU.subtract).then_inc(s_wa_lo, 1)

            def stats(s, n, par):
                if not live(n):
                    return
                if s == "f1":
                    dve.wait_ge(s_load[par], value(n * 8 + (16 - 8 * par)))
                elif s == "at":
                    dve.wait_ge(s_x["f1"], value(n + 1))
                else:
                    dve.wait_ge(A["x2"], value(n + 1))
                if due(n):
                    dve.wait_ge(s_nb[s], value(n))
                dve.sem_inc(s_gate, 1)
                for k in range(TG):
                    tile = x_sb[:, bass.ds(value(n * TG + k), 1), :].rearrange("p a d -> p (a d)")
                    i = v.bn_stats(bn[s][:, k, :], tile)
                i.then_inc(s_bn[s], 1)

            def mean_variance(s, n):
                if not live(n):
                    return
                dve.wait_ge(s_bn[s], value(n + 1))
                dve.sem_inc(s_gate, 1)
                for k in range(TG):
                    i = v.bn_aggr(mv[s][:, k, :], bn[s][:, k, :])
                i.then_inc(s_mv[s], 1)

            def high_part(s, n, par):
                if not live(n):
                    return
                u = par if nx[s] == 2 else 0
                dve.wait_ge(s_xT[s], value(n + 1))
                v.tensor_copy(x_hi[s][u][:], xT[s][:]).then_inc(s_hi[s], 1)

            def take_sigmoid(s, n, step):
                if not live(n):
                    return
                if step == 0:
                    dve.wait_ge(s_ex[s], value(n + 1))
                    v.tensor_scalar(r1[s][:], ex[s][:], 1.0, None, ALU.add).then_inc(s_rt[s], 1)
                elif step == 1:
                    dve.wait_ge(s_rt[s], value(n * RSTEPS + 1))
                    v.reciprocal(prob[s][:], r1[s][:]).then_inc(s_rt[s], 1)
                elif step == 2:
                    dve.wait_ge(s_rt[s], value(n * RSTEPS + 2))
                    for k in range(TG):
                        i = v.tensor_tensor(geq[s][:, k, :, :],
                                            prob[s][:, k, :].unsqueeze(1).to_broadcast([P, EXP, EXP]),
                                            prob[s][:, k, :].unsqueeze(2).to_broadcast([P, EXP, EXP]), ALU.is_ge)
                    i.then_inc(s_geq[s], 1)
                elif step == 3:
                    dve.wait_ge(s_geq[s], value(n + 1))
                    for k in range(TG):
                        i = v.tensor_tensor(ahead[s][:, k, :, 0:EXP], geq[s][:, k, :, :], before, ALU.mult)
                    i.then_inc(s_ahead[s], 1)

            def pick_two(s, n, step):
                if not live(n):
                    return
                if step == 0:
                    dve.wait_ge(s_ahead[s], value(n + 1))
                    v.reduce_sum(r1[s][:], ahead[s][:], axis=AX.X).then_inc(s_rt[s], 1)
                    for k in range(TG):
                        i = v.reduce_sum(r2[s][:, k, :], ahead[s][:, k, :, 0:EXP].rearrange("p a b -> p b a"),
                                         axis=AX.X)
                    i.then_inc(s_rt[s], 1)
                elif step == 1:
                    dve.wait_ge(s_rt[s], value(n * RSTEPS + 4))
                    v.tensor_tensor(r1[s][:], r1[s][:], r2[s][:], ALU.subtract).then_inc(s_rt[s], 1)
                elif step == 2:
                    dve.wait_ge(s_rt[s], value(n * RSTEPS + 5))
                    for k in range(TOPK):
                        i = v.scalar_tensor_tensor(pick[s][:, k], r1[s][:], float(k), prob[s][:],
                                                   ALU.is_equal, ALU.mult)
                    i.then_inc(s_rt[s], 1)
                elif step == 3:
                    dve.wait_ge(s_rt[s], value(n * RSTEPS + 6))
                    v.reduce_sum(p_top[s][:], pick[s][:], axis=AX.X).then_inc(s_rt[s], 1)
                elif step == 4:
                    dve.wait_ge(s_rt[s], value(n * RSTEPS + 7))
                    v.tensor_tensor(tot[s][:], p_top[s][:, 0], p_top[s][:, 1], ALU.add).then_inc(s_rt[s], 1)
                elif step == 5:
                    dve.wait_ge(s_rt[s], value(n * RSTEPS + 8))
                    v.tensor_scalar(tot[s][:], tot[s][:], 1e-20, 2.0, ALU.add, ALU.mult).then_inc(s_rt[s], 1)

            def weigh_two(s, n, step):
                if not live(n):
                    return
                if step == 0:
                    dve.wait_ge(s_rt[s], value(n * RSTEPS + RSTEPS))
                    v.reciprocal(rtot[s][:], tot[s][:]).then_inc(s_cw[s], 1)
                elif step == 1:
                    dve.wait_ge(s_cw[s], value(n * 3 + 1))
                    v.tensor_tensor(cw[s][:], p_top[s][:], rtot[s][:].unsqueeze(1).to_broadcast([P, TOPK, TG]),
                                    ALU.mult).then_inc(s_cw[s], 1)
                elif step == 2:
                    dve.wait_ge(s_cw[s], value(n * 3 + 2))
                    v.tensor_scalar(cwt[s][:], cw[s][:], TINY, None, ALU.max).then_inc(s_cw[s], 1)

            def spread_roots(s, n, step):
                if not live(n):
                    return
                if step == 0:
                    dve.wait_ge(s_root[s], value(n + 1))
                    v.scalar_tensor_tensor(g_top[s][:], cw[s][:], 0.0, root[s][:], ALU.is_gt, ALU.mult) \
                        .then_inc(s_gm[s], 1)
                elif step == 1:
                    dve.wait_ge(s_gm[s], value(n * 2 + 1))
                    for k in range(TOPK):
                        i = v.scalar_tensor_tensor(pick[s][:, k], r1[s][:], float(k),
                                                   g_top[s][:, k].unsqueeze(2).to_broadcast([P, TG, EXP]),
                                                   ALU.is_equal, ALU.mult)
                    i.then_inc(s_gm[s], 1)
                elif step == 2:
                    dve.wait_ge(s_gm[s], value(n * 2 + 2))
                    if due(n):
                        dve.wait_ge(s_ct[s], value(n))
                    v.tensor_tensor(g_tok[s][:].rearrange("p e k -> p k e"), pick[s][:, 0], pick[s][:, 1], ALU.add) \
                        .then_inc(s_gt[s], 1)

            def weighted(t, place):
                for s, n, c, ago in chunks(t, place):
                    if c % (NC // 2) == 0:
                        dve.wait_ge(s_ga[s][c // (NC // 2)], value(n * 16 + 16))
                    m = n * NC + (c - STAGE + 1)
                    if due(m):
                        dve.wait_ge(s_hlo[s], value(m))
                    m = turns(s, t - ago) * NC + (c - STAGE + 1)
                    if c < STAGE and due(m):
                        dve.wait_ge(s_hlo[other[s]], value(m))
                    dve.wait_ge(s_p1[s], value(n * NC + c + 1))
                    v.scalar_tensor_tensor(hid[:, c % STAGE, :], hp[c % 2][:], 0.0, g_all[s][:, EXPERT[c], :],
                                           ALU.max, ALU.mult).then_inc(s_z[s], 1)

            def add_moe(s, n, t0):
                if live(n):
                    y = yp[other[s] if alone(s, t0) else s]
                    dve.wait_ge(s_y[s], value(n + 1))
                    tiles = x_sb[:, bass.ds(value(n * TG), TG), :]
                    v.tensor_tensor(tiles, y[:].rearrange("p (k d) -> p k d", k=TG), tiles, ALU.add) \
                        .then_inc(s_x[s], 1)

            def rope_q_cos(n):
                if live(n):
                    dve.wait_ge(A["q"], value(n + 1))
                    if due(n):
                        dve.wait_ge(A["qf"], value(n))
                    v.tensor_tensor(qa[:], a0[:].rearrange("p (b t) -> p b t", b=BG), cos_q, ALU.mult).then_inc(A["qa"], 1)

            def rope_q_sin(n):
                if not live(n):
                    return
                dve.wait_ge(A["qr"], value(n + 1))
                v.tensor_tensor(qb[:], a1[:].rearrange("p (b t) -> p b t", b=BG), sin_q, ALU.mult).then_inc(A["qb"], 1)

            def rope_q_sum(n):
                if not live(n):
                    return
                dve.wait_ge(A["qb"], value(n + 1))
                v.scalar_tensor_tensor(qa[:], qa[:], 1.0, qb[:], ALU.add, ALU.add).then_inc(A["xq"], 1)

            def q_features(n):
                if live(n):
                    dve.wait_ge(A["eq"], value(n + 1))
                    if due(n):
                        dve.wait_ge(A["nd"], value(n))
                    v.scalar_tensor_tensor(qf[:].rearrange("p (b t) -> p b t", b=BG), eq[:], 1.0, qa[:], ALU.min, ALU.max) \
                        .then_inc(A["qf"], 1)

            def rope_k(n, b):
                if not live(n):
                    return
                dve.wait_ge(A["kv"], value(n * BG + b + 1))
                if b == 0:
                    if due(n):
                        dve.wait_ge(A["kf"], value(n))
                k = (a2, a0)[b][:].rearrange("p (r c) -> p r c", r=RT)[:, :, 0:D]
                tiles = slice(b * RT, (b + 1) * RT)
                v.tensor_tensor(ka[:, tiles, :], k, cos_k, ALU.mult).then_inc(A["ka"], 1)
                swapped = k.rearrange("p r (w c) -> p r w c", w=2)[:, :, ::-1, :]
                v.tensor_tensor(kb[:, tiles, :].rearrange("p r (w c) -> p r w c", w=2), swapped,
                                sin_k.rearrange("p r (w c) -> p r w c", w=2), ALU.mult).then_inc(A["kb"], 1)

            def rope_k_sum(n):
                if live(n):
                    dve.wait_ge(A["kb"], value(n * BG + BG))
                    v.scalar_tensor_tensor(ka[:], ka[:], 1.0, kb[:], ALU.add, ALU.add).then_inc(A["xk"], 1)

            def k_features(n):
                if live(n):
                    dve.wait_ge(A["ek"], value(n + 1))
                    v.scalar_tensor_tensor(kf[:], ek[:], 1.0, ka[:], ALU.min, ALU.max).then_inc(A["kf"], 1)

            def mask_state(n):
                if not live(n):
                    return
                dve.wait_ge(A["state"], value(n + 1))
                st = a1[:].rearrange("p (b c) -> p b c", b=BG)
                v.tensor_tensor(kvm[:, :, 0:D], st[:, :, 0:D], same_head, ALU.mult).then_inc(A["kvm"], 1)
                v.tensor_tensor(kvm[:, :, D:KVW], st[:, :, D:D + 1].to_broadcast([P, BG, HEADS]), in_head, ALU.mult) \
                    .then_inc(A["kvs"], 1)

            def normalise(n, step):
                if not live(n):
                    return
                if step == 0:
                    dve.wait_ge(A["nd"], value(n + 1))
                    for b in range(BG):
                        nd = (a2, a0)[b][:].rearrange("p (r c) -> p r c", r=RT)
                        i = v.tensor_scalar(den[:, b * RT:(b + 1) * RT, :], nd[:, :, D:KVW], 1e-6, None, ALU.max)
                    i.then_inc(A["den"], 1)
                elif step == 1:
                    dve.wait_ge(A["den"], value(n + 1))
                    v.reciprocal(rden[:], den[:]).then_inc(A["rden"], 1)
                elif step == 2:
                    dve.wait_ge(A["rden"], value(n + 1))
                    for b in range(BG):
                        nd = (a2, a0)[b][:].rearrange("p (r c) -> p r c", r=RT)
                        i = v.tensor_tensor(attn[:, b * RT:(b + 1) * RT, :].rearrange("p r (h c) -> p r h c", h=HEADS),
                                            nd[:, :, 0:D].rearrange("p r (h c) -> p r h c", h=HEADS),
                                            rden[:, b * RT:(b + 1) * RT, :].unsqueeze(3)
                                            .to_broadcast([P, RT, HEADS, HD]), ALU.mult)
                    i.then_inc(A["attn"], 1)

            def add_attention(n):
                if live(n):
                    dve.wait_ge(A["y"], value(n + 1))
                    tiles = x_sb[:, bass.ds(value(n * TG), TG), :]
                    v.tensor_tensor(tiles, a2[:].rearrange("p (k d) -> p k d", k=TG), tiles, ALU.add).then_inc(A["x2"], 1)

            def iteration(t, par):
                p2 = (par + SHIFT) % 2
                n1, n2, n2_last = t + 2, t + 2 - SHIFT, t + 1 - SHIFT
                if first_time(True, t + 1):
                    split_attention_weights()
                if alone("f2", t - 2):
                    add_moe("f2", t - 1 - SHIFT, t - 2)
                k_features(t - 2)
                weighted(t, 0)
                high_part("f1", n1, par)
                spread_roots("f2", n2_last, 0)
                weighted(t, 1)
                spread_roots("f2", n2_last, 1)
                q_features(t - 2)
                weighted(t, 2)
                spread_roots("f2", n2_last, 2)
                if not alone("f1", t - 1):
                    add_moe("f1", t, t - 1)
                weighted(t, 3)
                take_sigmoid("f1", n1, 0)
                stats("f1", t + 3, (par + 1) % 2)
                weighted(t, 4)
                take_sigmoid("f1", n1, 1)
                mean_variance("f1", t + 3)
                if first_time(True, t + 3):
                    set_ranks()
                    split_w1()
                mask_state(t - 2)
                weighted(t, 5)
                take_sigmoid("f1", n1, 2)
                weighted(t, 6)
                take_sigmoid("f1", n1, 3)
                weighted(t, 7)
                normalise(t - 2, 0)
                pick_two("f1", n1, 0)
                weighted(t, 8)
                normalise(t - 2, 1)
                pick_two("f1", n1, 1)
                weighted(t, 9)
                normalise(t - 2, 2)
                pick_two("f1", n1, 2)
                weighted(t, 10)
                high_part("at", t - 1, 0)
                pick_two("f1", n1, 3)
                pick_two("f1", n1, 4)
                weighted(t, 11)
                pick_two("f1", n1, 5)
                weigh_two("f1", n1, 0)
                weigh_two("f1", n1, 1)
                weigh_two("f1", n1, 2)
                weighted(t, 12)
                high_part("f2", n2, p2)
                spread_roots("f1", n1, 0)
                weighted(t, 13)
                spread_roots("f1", n1, 1)
                weighted(t, 14)
                if alone("f1", t - 1):
                    add_moe("f1", t, t - 1)
                spread_roots("f1", n1, 2)
                if not alone("f2", t - 1):
                    add_moe("f2", t - SHIFT, t - 1)
                weighted(t, 15)
                take_sigmoid("f2", n2, 0)
                rope_q_cos(t - 1)
                weighted(t, 16)
                take_sigmoid("f2", n2, 1)
                stats("at", t, 0)
                weighted(t, 17)
                take_sigmoid("f2", n2, 2)
                mean_variance("at", t)
                weighted(t, 18)
                take_sigmoid("f2", n2, 3)
                add_attention(t - 2)
                weighted(t, 19)
                rope_q_sin(t - 1)
                pick_two("f2", n2, 0)
                weighted(t, 20)
                rope_q_sum(t - 1)
                stats("f2", t + 3 - SHIFT, 0)
                pick_two("f2", n2, 1)
                weighted(t, 21)
                mean_variance("f2", t + 3 - SHIFT)
                pick_two("f2", n2, 2)
                rope_k(t - 1, 0)
                weighted(t, 22)
                pick_two("f2", n2, 3)
                rope_k(t - 1, 1)
                pick_two("f2", n2, 4)
                weighted(t, 23)
                rope_k_sum(t - 1)
                pick_two("f2", n2, 5)
                weigh_two("f2", n2, 0)
                weigh_two("f2", n2, 1)
                weigh_two("f2", n2, 2)

            pipeline(dve, iteration)


_INS = ["x", "wqkv", "wout", "router", "w1", "w2", "const"]


def kernel(L0_attn_x, L0_attn_W_qkv, L0_attn_W_out, L0_ffn_router_w, L0_ffn_w1, L0_ffn_w2):
    import concourse.bacc as bacc
    from concourse.bass_utils import run_bass_kernel_spmd

    w = np.asarray(L0_attn_W_qkv).reshape(D, 3, HEADS, 2, HALF)
    qk = w[:, 0:2].transpose(0, 1, 3, 2, 4).reshape(D, 2 * D)
    arrays = {
        "x": np.ascontiguousarray(L0_attn_x),
        "wqkv": np.ascontiguousarray(np.concatenate([qk, w[:, 2].reshape(D, D)], 1)),
        "wout": np.ascontiguousarray(L0_attn_W_out),
        "router": np.ascontiguousarray(np.asarray(L0_ffn_router_w).T),
        "w1": np.ascontiguousarray(L0_ffn_w1),
        "w2": np.ascontiguousarray(L0_ffn_w2),
        "const": CONST,
    }
    nc = bacc.Bacc("TRN2", target_bir_lowering=False, num_devices=1,
                   dynamic_dma_scratch_size=1024)
    aps = [nc.dram_tensor(f"in_{n}", arrays[n].shape, F32, kind="ExternalInput").ap() for n in _INS]
    out = nc.dram_tensor("out_x", (B, T, D), F32, kind="ExternalOutput").ap()
    rows = {s: nc.dram_tensor(f"rows_{s}", (EXP, NTOK), F32).ap() for s in ("f1", "f2")}
    build(nc, *aps, out, rows)
    r = run_bass_kernel_spmd(nc, [{f"in_{n}": arrays[n] for n in _INS}], core_ids=[0])
    return r.results[0]["out_x"]
```
